# Optimizing a Trainium2 kernel written in Bass

```python
import numpy as np
import jax
import jax.numpy as jnp

def _softmax(x, axis=-1):
    return jax.nn.softmax(x, axis=axis)

def _gelu(x):
    return jax.nn.gelu(x, approximate=True)

def _silu(x):
    return jax.nn.silu(x)

def _sigmoid(x):
    return jax.nn.sigmoid(x)

def _layernorm(x, axis=-1, eps=1e-05):
    m = jnp.mean(x, axis=axis, keepdims=True)
    v = jnp.var(x, axis=axis, keepdims=True)
    return (x - m) / jnp.sqrt(v + eps)

def _scatter_add(tgt, idx, src, axis=0):
    return tgt.at[idx].add(src)

def _segment_sum(src, seg, n):
    return jax.ops.segment_sum(src, seg, n)
kernel_name = 'mk_gnn_preln_d1_gnn_r8_7851a4'

def setup_inputs(seed: int=0):
    np.random.seed(seed)
    _w = jnp.asarray

    def _rec_inputs():
        import jax
        import jax.numpy as jnp
        _gk = jax.random.key(seed)
        x = -0.000202 + 1 * jax.random.normal(jax.random.fold_in(_gk, 1), (12500, 128), jnp.float32)
        src = jax.random.randint(jax.random.fold_in(_gk, 2), (200000,), 0, 12500, jnp.int32)
        dst = jnp.minimum((12500 * jax.random.uniform(jax.random.fold_in(_gk, 3), (200000,)) ** 2.0).astype(jnp.int32), 99999)
        _o = jnp.argsort(dst, stable=True)
        src = src[_o]
        dst = dst[_o]
        return (x, src, dst)
    x, src, dst = _rec_inputs()

    def _L0_gnn_setup():
        import jax, jax.numpy as jnp
        import numpy as np
        N, E = (6250, 100000)
        IN_C, HID, OUT_C = (128, 256, 128)
        EPS = 1e-05

        def _sage_conv(x, src, dst, Wl, bl, Wr):
            agg = jax.ops.segment_sum(x[src], dst, num_segments=x.shape[0])
            deg = jax.ops.segment_sum(jnp.ones_like(dst, dtype=x.dtype), dst, num_segments=x.shape[0])
            mean = agg / jnp.maximum(deg, 1.0)[:, None]
            return mean @ Wl + bl + x @ Wr

        def _batchnorm(x, g, b):
            m = jnp.mean(x, axis=0)
            v = jnp.mean((x - m) ** 2, axis=0)
            return (x - m) * jax.lax.rsqrt(v + EPS) * g + b
        key = jax.random.key(seed)
        ks = jax.random.split(key, 16)
        x = jax.random.normal(ks[0], (N, IN_C), dtype=jnp.float32)
        edge_index = jax.random.randint(ks[1], (2, E), 0, N, dtype=jnp.int64)

        def lin(k, fan_in, fan_out):
            bound = 1.0 / np.sqrt(fan_in)
            return jax.random.uniform(k, (fan_in, fan_out), jnp.float32, -bound, bound)
        return {'x': x, 'edge_index': edge_index, 'Wl0': lin(ks[2], IN_C, HID), 'bl0': jnp.zeros((HID,), jnp.float32), 'Wr0': lin(ks[3], IN_C, HID), 'g0': jnp.ones((HID,), jnp.float32), 'b0': jnp.zeros((HID,), jnp.float32), 'Wl1': lin(ks[4], HID, HID), 'bl1': jnp.zeros((HID,), jnp.float32), 'Wr1': lin(ks[5], HID, HID), 'g1': jnp.ones((HID,), jnp.float32), 'b1': jnp.zeros((HID,), jnp.float32), 'Wl2': lin(ks[6], HID, OUT_C), 'bl2': jnp.zeros((OUT_C,), jnp.float32), 'Wr2': lin(ks[7], HID, OUT_C)}
    _L0_gnn_all = _L0_gnn_setup()
    _L0_gnn_in = {k: v for k, v in _L0_gnn_all.items() if k in ('Wl0', 'bl0', 'Wr0', 'g0', 'b0', 'Wl1', 'bl1', 'Wr1', 'g1', 'b1', 'Wl2', 'bl2', 'Wr2')}
    del _L0_gnn_all
    return {'x': x, 'src': src, 'dst': dst, 'L0_gnn_Wl0': _L0_gnn_in['Wl0'], 'L0_gnn_bl0': _L0_gnn_in['bl0'], 'L0_gnn_Wr0': _L0_gnn_in['Wr0'], 'L0_gnn_g0': _L0_gnn_in['g0'], 'L0_gnn_b0': _L0_gnn_in['b0'], 'L0_gnn_Wl1': _L0_gnn_in['Wl1'], 'L0_gnn_bl1': _L0_gnn_in['bl1'], 'L0_gnn_Wr1': _L0_gnn_in['Wr1'], 'L0_gnn_g1': _L0_gnn_in['g1'], 'L0_gnn_b1': _L0_gnn_in['b1'], 'L0_gnn_Wl2': _L0_gnn_in['Wl2'], 'L0_gnn_bl2': _L0_gnn_in['bl2'], 'L0_gnn_Wr2': _L0_gnn_in['Wr2']}

def reference(x, src, dst, L0_gnn_Wl0, L0_gnn_bl0, L0_gnn_Wr0, L0_gnn_g0, L0_gnn_b0, L0_gnn_Wl1, L0_gnn_bl1, L0_gnn_Wr1, L0_gnn_g1, L0_gnn_b1, L0_gnn_Wl2, L0_gnn_bl2, L0_gnn_Wr2):
    import jax
    import jax.numpy as jnp

    def _L0_gnn_ref(x, edge_index, Wl0, bl0, Wr0, g0, b0, Wl1, bl1, Wr1, g1, b1, Wl2, bl2, Wr2):
        import jax, jax.numpy as jnp
        import numpy as np
        N, E = (6250, 100000)
        IN_C, HID, OUT_C = (128, 256, 128)
        EPS = 1e-05

        def _sage_conv(x, src, dst, Wl, bl, Wr):
            agg = jax.ops.segment_sum(x[src], dst, num_segments=x.shape[0])
            deg = jax.ops.segment_sum(jnp.ones_like(dst, dtype=x.dtype), dst, num_segments=x.shape[0])
            mean = agg / jnp.maximum(deg, 1.0)[:, None]
            return mean @ Wl + bl + x @ Wr

        def _batchnorm(x, g, b):
            m = jnp.mean(x, axis=0)
            v = jnp.mean((x - m) ** 2, axis=0)
            return (x - m) * jax.lax.rsqrt(v + EPS) * g + b
        src, dst = (edge_index[0], edge_index[1])
        h = _sage_conv(x, src, dst, Wl0, bl0, Wr0)
        h = jax.nn.relu(_batchnorm(h, g0, b0))
        h = _sage_conv(h, src, dst, Wl1, bl1, Wr1)
        h = jax.nn.relu(_batchnorm(h, g1, b1))
        return _sage_conv(h, src, dst, Wl2, bl2, Wr2)
    edge_index = jnp.stack([src, dst])
    h = jnp.maximum(_layernorm(x, axis=-1), 0.0)
    x = x + _L0_gnn_ref(h, edge_index, L0_gnn_Wl0, L0_gnn_bl0, L0_gnn_Wr0, L0_gnn_g0, L0_gnn_b0, L0_gnn_Wl1, L0_gnn_bl1, L0_gnn_Wr1, L0_gnn_g1, L0_gnn_b1, L0_gnn_Wl2, L0_gnn_bl2, L0_gnn_Wr2)
    return x

_drawn_inputs = setup_inputs


def setup_inputs(seed=0):
    import zlib

    import numpy as np

    out = dict(_drawn_inputs(seed))
    spreads = {'L0_gnn_bl0': (0.0, 0.1),
     'L0_gnn_g0': (1.0, 0.2),
     'L0_gnn_b0': (0.0, 0.1),
     'L0_gnn_bl1': (0.0, 0.1),
     'L0_gnn_g1': (1.0, 0.2),
     'L0_gnn_b1': (0.0, 0.1),
     'L0_gnn_bl2': (0.0, 0.1)}
    factors = {}
    for name, (base, spread) in spreads.items():
        noise = np.random.default_rng([zlib.crc32(name.encode()), seed]).standard_normal(out[name].shape)
        drawn = base * np.exp(spread * noise) if base else spread * noise
        out[name] = jnp.asarray(drawn.astype(out[name].dtype))
    for name, factor in factors.items():
        out[name] = (out[name] * factor).astype(out[name].dtype)
    return out
```

```python
import concourse.bass as bass
from concourse import mybir
from contextlib import ExitStack

P = 128
NODES = 12500
EDGES = 200000
IN_C, HID, OUT_C = 128, 256, 128
EPS = 1e-5

BLOCKS = -(-NODES // P)
PADDED = BLOCKS * P
LAST_ROWS = NODES - (BLOCKS - 1) * P
TILES = -(-EDGES // P)
WALK = TILES + BLOCKS - 1
KCH = -(-WALK // P)
STEPS = KCH * P
HALF = 8
PER_IT = 2 * HALF
ITERS = STEPS // PER_IT
TAB_ROWS = STEPS
PAD_EDGES = TAB_ROWS * P - EDGES
NO_NODE = 1 << 20
CH = 2 * P
CHUNKS = PADDED // CH
LAST_COLS = NODES - (CHUNKS - 1) * CH


def gnn_kernel(nc, x, src, dst, Wl0, bl0, Wr0, g0, b0, Wl1, bl1, Wr1, g1, b1, Wl2, bl2, Wr2, out):
    f32 = mybir.dt.float32
    i32 = mybir.dt.int32
    u32 = mybir.dt.uint32
    ALU = mybir.AluOpType
    ACT = mybir.ActivationFunctionType
    ds = bass.ds

    ctx = ExitStack()
    with ctx:
        def sb(name, shape, dt=f32):
            return ctx.enter_context(nc.sbuf_tensor(name, shape, dt))

        def sem(name):
            return ctx.enter_context(nc.semaphore(name))

        def dram(name, shape, dt=f32):
            return nc.dram_tensor(name, shape, dt, kind="Internal").ap()

        src_tab = dram("src_tab", [TAB_ROWS, P], i32)
        dst_tab = dram("dst_tab", [TAB_ROWS, P], i32)
        block_dram = dram("block_dram", [STEPS], i32)
        table = [dram("table0", [PADDED, IN_C]), dram("table1", [PADDED, HID]), dram("table2", [PADDED, OUT_C])]
        inv_dram = dram("inv_dram", [PADDED])
        self_dram = dram("self_dram", [P, 2, PADDED])

        big = sb("big", [P, 3, PADDED])
        ring = sb("ring", [P, PER_IT, HID])
        onehot = sb("onehot", [P, PER_IT, P])
        idx_all = sb("idx_all", [P, STEPS], i32)
        rel_all = sb("rel_all", [P, STEPS])
        block_row = sb("block_row", [1, STEPS], i32)
        idx_now = sb("idx_now", [P, 2, HALF], i32)
        w0 = sb("w0", [P, 2, HID])
        w1 = sb("w1", [P, 2, 2, HID])
        w2 = sb("w2", [P, 2, 2 * OUT_C])
        cols = sb("cols", [P, 6, 2])
        bl2_all = sb("bl2_all", [P, OUT_C])
        iota_row = sb("iota_row", [P, P])
        part_col = sb("part_col", [P, 1])
        ident = sb("ident", [P, P])
        ones = sb("ones", [P, P])
        zeros = sb("zeros", [P, 1, CH])
        block_end = sb("block_end", [P, BLOCKS - 1])
        block_no = sb("block_no", [P, BLOCKS - 1])
        step_no = sb("step_no", [P, KCH])
        pads = sb("pads", [P, 2, P], i32)
        firsts = sb("firsts", [P, KCH], i32)
        firsts_f = sb("firsts_f", [P, KCH])
        ends = sb("ends", [P, BLOCKS - 1])
        block_of = sb("block_of", [P, KCH])
        first_node = sb("first_node", [P, KCH])
        first_node_i = sb("first_node_i", [P, KCH], i32)
        tile_no = sb("tile_no", [P, KCH], i32)
        stats = sb("stats", [P, 2 * CHUNKS, 6])
        rstd = sb("rstd", [P, BLOCKS])
        inv_col = sb("inv_col", [P, BLOCKS])
        bn_mv = sb("bn_mv", [P, 2, 2])
        bn_scale = sb("bn_scale", [P, 2])
        bn_shift = sb("bn_shift", [P, 2])
        bn_tmp = sb("bn_tmp", [P, 2])

        row_stage = ring[:, 0:4, :].rearrange("p (u j) c -> p u j c", u=2)
        self_stage = ring[:, 4:8, :].rearrange("p (u j) c -> p u j c", u=2)
        h_stage = ring[:, 8:12, :].rearrange("p (u j) c -> p u j c", u=2)
        src_nat = big[:, 2, 0:STEPS].bitcast(i32)
        dst_nat = big[:, 2, STEPS:2 * STEPS].bitcast(i32)
        src_f = big[:, 2, 2 * STEPS:3 * STEPS]
        rel_f = big[:, 2, 3 * STEPS:4 * STEPS]
        starts_below = big[:, 2, 4 * STEPS:4 * STEPS + KCH * (BLOCKS - 1)].rearrange("p (c b) -> p c b", c=KCH)
        below = big[:, 2, 6 * STEPS:6 * STEPS + KCH * (BLOCKS - 1)].rearrange("p (c b) -> p c b", c=KCH)
        res = big[:, 2, :].rearrange("p (b f) -> p b f", f=OUT_C)
        scratch = 6 * STEPS + KCH * (BLOCKS - 1)
        mv = big[:, 2, scratch:scratch + 2 * BLOCKS].rearrange("p (b s) -> p b s", s=2)
        nbias = big[:, 2, scratch + 2 * BLOCKS:scratch + 3 * BLOCKS]
        x_nat = big[:, 1, :].rearrange("p (b f) -> p b f", f=IN_C)

        ps = ctx.enter_context(nc.psum_tensor("ps", [P, 8, 512], f32))

        s_const = sem("s_const")
        s_pads = sem("s_pads")
        s_weights = sem("s_weights")
        s_x = sem("s_x")
        s_tabs = sem("s_tabs")
        s_firsts = sem("s_firsts")
        s_cmp = sem("s_cmp")
        s_counts = sem("s_counts")
        s_ids = sem("s_ids")
        s_brow_out = sem("s_brow_out")
        s_brow = sem("s_brow")
        s_nat = sem("s_nat")
        s_natf = sem("s_natf")
        s_edgeT = sem("s_edgeT")
        s_edges = sem("s_edges")
        s_dve = sem("s_dve")
        s_lnst = sem("s_lnst")
        s_var = sem("s_var")
        s_sd = sem("s_sd")
        s_lncoef = sem("s_lncoef")
        s_h0 = sem("s_h0")
        s_h0T = sem("s_h0T")
        s_h0ev = sem("s_h0ev")
        s_h0_out = [sem(f"s_h0_out{u}") for u in range(2)]
        s_tables = sem("s_tables")
        s_zero = sem("s_zero")
        s_idx = sem("s_idx")
        s_half = sem("s_half")
        s_rows = [sem(f"s_rows{h}") for h in range(2)]
        s_hot = sem("s_hot")
        s_sum = sem("s_sum")
        s_acc = sem("s_acc")
        s_mean = sem("s_mean")
        s_inv = sem("s_inv")
        s_inv_out = sem("s_inv_out")
        s_inv_col = sem("s_inv_col")
        s_zmm = sem("s_zmm")
        s_z = sem("s_z")
        s_bnst = sem("s_bnst")
        s_bnvar = sem("s_bnvar")
        s_bnsd = sem("s_bnsd")
        s_bn = sem("s_bn")
        s_h = sem("s_h")
        s_rowmm = sem("s_rowmm")
        s_selfmm = sem("s_selfmm")
        s_rowev = sem("s_rowev")
        s_selfev = sem("s_selfev")
        s_row_out = [sem(f"s_row_out{u}") for u in range(2)]
        s_self_out = [sem(f"s_self_out{u}") for u in range(2)]
        s_self_in = [sem(f"s_self_in{u}") for u in range(2)]
        s_zadd = sem("s_zadd")
        s_h2 = sem("s_h2")
        s_pmm = sem("s_pmm")
        s_pev = sem("s_pev")
        s_p_out = [sem(f"s_p_out{u}") for u in range(2)]
        s_x2 = [sem(f"s_x2{u}") for u in range(2)]
        s_x2b = sem("s_x2b")
        s_r2 = sem("s_r2")
        s_fin = sem("s_fin")
        s_out = sem("s_out")

        EVEN, ODD = (CHUNKS + 1) // 2, CHUNKS // 2

        def each_chunk(eng, body, peeled=1):
            for t in range(peeled):
                body(2 * t, 0, t)
                body(2 * t + 1, 1, t)
            with eng.Fori(peeled, CHUNKS // 2) as t:
                for u in range(2):
                    body(t * 2 + u, u, t)
            body(CHUNKS - 1, 0, CHUNKS // 2)

        def wait(eng, s, value):
            if not isinstance(value, int) or value > 0:
                eng.wait_ge(s, value)

        def last_chunk(n):
            return isinstance(n, int) and n == CHUNKS - 1

        block = ctx.enter_context(nc.Block())

        @block.sync
        def _(sp):
            flat = [tab.rearrange("t e -> (t e)") for tab in (src_tab, dst_tab)]
            for tab, edges in zip(flat, (src, dst)):
                sp.dma_start(tab[0:EDGES].rearrange("(a n) -> a n", a=16),
                             edges.rearrange("(a n) -> a n", a=16)).then_inc(s_tabs, 16)
            full = PAD_EDGES // P
            left = PAD_EDGES - full * P
            sp.wait_ge(s_pads, 3)
            for k, tab in enumerate(flat):
                sp.dma_start(tab[EDGES:EDGES + full * P].rearrange("(a n) -> a n", n=P),
                             pads[0:full, k, :]).then_inc(s_tabs, 16)
                sp.dma_start(tab[EDGES + full * P:EDGES + full * P + left].rearrange("(a n) -> a n", a=1),
                             pads[0:1, k, 0:left]).then_inc(s_tabs, 16)
            xb = x[0:(BLOCKS - 1) * P, :].rearrange("(b p) f -> p b f", p=P)
            sp.dma_start(x_nat[:, 0:BLOCKS - 1, :], xb).then_inc(s_x, 16)
            sp.dma_start(x_nat[0:LAST_ROWS, BLOCKS - 1, :], x[(BLOCKS - 1) * P:NODES, :]).then_inc(s_x, 16)
            sp.wait_ge(s_tabs, 16 * 6)
            with nc.allow_non_contiguous_dma(reason="one word of each tile"):
                sp.dma_start(firsts[:, :], dst_tab[:, 0].rearrange("(c p) -> p c", p=P)).then_inc(s_firsts, 16)
            sp.wait_ge(s_ids, 1)
            with nc.allow_non_contiguous_dma(reason="one word a step"):
                sp.dma_start(block_dram.rearrange("(c p) -> p c", p=P), first_node_i[:, :]).then_inc(s_brow_out, 16)
            sp.wait_ge(s_brow_out, 16)
            sp.dma_start(block_row[0:1, :], block_dram.rearrange("(a n) -> a n", a=1)).then_inc(s_brow, 16)

            tb0 = table[0].rearrange("(b p) f -> p b f", p=P)

            def store_h0(n, u, t):
                sp.wait_ge(s_h0, (n + 1) * 2)
                sp.dma_start(tb0[:, ds(n * 2, 2), :],
                             h_stage[:, u].rearrange("p j c -> p (j c)")[:, 0:CH].rearrange("p (j f) -> p j f", j=2)
                             ).then_inc(s_h0_out[u], 16)
            each_chunk(sp, store_h0)
            sp.wait_ge(s_h0_out[0], 16 * EVEN)
            sp.wait_ge(s_h0_out[1], 16 * ODD)
            sp.sem_inc(s_tables, 1)

            sp.wait_ge(s_inv, 1)
            sp.dma_start(inv_dram.rearrange("(a n) -> a n", a=1), big[0:1, 2, :]).then_inc(s_inv_out, 16)
            sp.wait_ge(s_inv_out, 16)
            with nc.allow_non_contiguous_dma(reason="one word a node"):
                sp.dma_start(inv_col[:, :], inv_dram.rearrange("(b p) -> p b", p=P)).then_inc(s_inv_col, 16)

            tb1 = table[1].rearrange("(b p) f -> p b f", p=P)

            def store_1(n, u, t):
                sp.wait_ge(s_rowev, n + 1)
                sp.dma_start(tb1[:, ds(n * 2, 2), :], row_stage[:, u]).then_inc(s_row_out[u], 16)
                sp.wait_ge(s_selfev, (n + 1) * 2)
                sp.dma_start(self_dram[:, :, ds(n * CH, CH)], self_stage[:, u]).then_inc(s_self_out[u], 16)
            each_chunk(sp, store_1)
            for s in (s_row_out, s_self_out):
                sp.wait_ge(s[0], 16 * EVEN)
                sp.wait_ge(s[1], 16 * ODD)
            sp.sem_inc(s_tables, 1)

            sp.wait_ge(s_sum, 2 + 2 * 2 * ITERS)

            def load_self(n, u, t):
                wait(sp, s_zadd, (n - 1) * 2)
                sp.dma_start(self_stage[:, u], self_dram[:, :, ds(n * CH, CH)]).then_inc(s_self_in[u], 16)
            each_chunk(sp, load_self)

            tb2 = table[2].rearrange("(b p) f -> p b f", p=P)

            def load_x_store_2(n, u, t):
                wait(sp, s_r2, n - 1)
                if last_chunk(n):
                    sp.dma_start(row_stage[:, u, 1, 0:P], x[n * CH:n * CH + P, :]).then_inc(s_x2[u], 16)
                    sp.dma_start(row_stage[0:LAST_ROWS, u, 1, P:2 * P], x[n * CH + P:NODES, :]).then_inc(s_x2[u], 16)
                else:
                    sp.dma_start(row_stage[:, u, 1, :].rearrange("p (j f) -> p j f", j=2),
                                 x[ds(n * CH, CH), :].rearrange("(j p) f -> p j f", p=P)).then_inc(s_x2[u], 16)
                sp.wait_ge(s_pev, n + 1)
                sp.dma_start(tb2[:, ds(n * 2, 2), :],
                             row_stage[:, u, 0, :].rearrange("p (j f) -> p j f", j=2)).then_inc(s_p_out[u], 16)
            each_chunk(sp, load_x_store_2)
            sp.wait_ge(s_p_out[0], 16 * EVEN)
            sp.wait_ge(s_p_out[1], 16 * ODD)
            sp.sem_inc(s_tables, 1)

            def store_out(n, u, t):
                sp.wait_ge(s_fin, (n + 1) * 2)
                if last_chunk(n):
                    sp.dma_start(out[n * CH:n * CH + P, :], res[:, 2 * n, :]).then_inc(s_out, 16)
                    sp.dma_start(out[n * CH + P:NODES, :], res[0:LAST_ROWS, 2 * n + 1, :]).then_inc(s_out, 16)
                else:
                    sp.dma_start(out[ds(n * CH, CH), :].rearrange("(j p) f -> p j f", p=P),
                                 res[:, ds(n * 2, 2), :]).then_inc(s_out, 16)
            each_chunk(sp, store_out)
            sp.wait_ge(s_out, 16 * (CHUNKS + 1))

        @block.gpsimd
        def _(pool):
            pool.memset(pads[:, 0, :], 0).then_inc(s_pads, 1)
            pool.memset(pads[:, 1, :], NO_NODE).then_inc(s_pads, 1)
            pool.memset(x_nat[:, BLOCKS - 1, :], 0.0).then_inc(s_pads, 1)
            f = dict(allow_small_or_imprecise_dtypes=True)
            pool.iota(iota_row[:, :], [[1, P]], base=0, channel_multiplier=0, **f).then_inc(s_const, 1)
            pool.iota(part_col[:, :], [[0, 1]], base=0, channel_multiplier=1, **f).then_inc(s_const, 1)
            pool.iota(block_end[:, :], [[P, BLOCKS - 1]], base=P, channel_multiplier=0, **f).then_inc(s_const, 1)
            pool.iota(block_no[:, :], [[1, BLOCKS - 1]], base=0, channel_multiplier=0, **f).then_inc(s_const, 1)
            pool.iota(step_no[:, :], [[P, KCH]], base=0, channel_multiplier=1, **f).then_inc(s_const, 1)
            pool.memset(ones[:, :], 1.0).then_inc(s_const, 1)
            pool.memset(zeros[:, :, :], 0.0).then_inc(s_const, 1)

            pool.wait_ge(s_ids, 1)
            for c in range(KCH):
                for tab, nat in ((src_tab, src_nat), (dst_tab, dst_nat)):
                    pool.indirect_dma_start(
                        out=nat[:, c * P:(c + 1) * P], out_offset=None, in_=tab[:, :],
                        in_offset=bass.IndirectOffsetOnAxis(ap=tile_no[:, c:c + 1].bitcast(u32), axis=0),
                    ).then_inc(s_nat, 16)

            for layer in range(3):
                width = table[layer].shape[1]
                pool.wait_ge(s_tables, layer + 1)
                with pool.Fori(0, ITERS) as i:
                    for h in range(2):
                        pool.wait_ge(s_idx, i * 2 + (2 * ITERS * layer + h + 1))
                        pool.sem_inc(s_half, 1)
                        for j in range(HALF):
                            pool.indirect_dma_start(
                                out=ring[:, h * HALF + j, 0:width], out_offset=None, in_=table[layer][:, :],
                                in_offset=bass.IndirectOffsetOnAxis(ap=idx_now[:, h, j:j + 1].bitcast(u32), axis=0),
                            ).then_inc(s_rows[h], 16)

        @block.scalar
        def _(act):
            for k, w in enumerate((Wl0, Wr0)):
                act.dma_start(w0[:, k, :], w).then_inc(s_weights, 16)
            for k, w in enumerate((Wl1, Wr1)):
                act.dma_start(w1[:, k], w.rearrange("(k p) n -> p k n", p=P)).then_inc(s_weights, 16)
            for k, w in enumerate((Wl2, Wr2)):
                act.dma_start(w2[:, :, k * OUT_C:(k + 1) * OUT_C],
                              w.rearrange("(k p) n -> p k n", p=P)).then_inc(s_weights, 16)
            with nc.allow_non_contiguous_dma(reason="vectors over the features"):
                for k, v in enumerate((bl0, g0, b0, bl1, g1, b1)):
                    act.dma_start(cols[:, k, :], v.rearrange("(m p) -> p m", p=P)).then_inc(s_weights, 16)
            act.dma_start(bl2_all[:, :], bl2.rearrange("(a n) -> a n", a=1).to_broadcast([P, OUT_C])).then_inc(s_weights, 16)

            act.wait_ge(s_var, 1)
            nc.scalar.activation(rstd[:, :], rstd[:, :], ACT.Sqrt).then_inc(s_sd, 1)
            act.wait_ge(s_lncoef, 1)

            def normalise(n, u, t):
                wait(act, s_h0T, n - 1)
                wait(act, s_h0_out[u], t * 16)
                for j in range(2):
                    b = n * 2 + j
                    nc.scalar.activation(h_stage[:, u, 0, j * P:(j + 1) * P],
                                         x_nat[:, ds(b, 1), :].rearrange("p a f -> p (a f)"), ACT.Relu,
                                         bias=nbias[:, ds(b, 1)], scale=rstd[:, ds(b, 1)]).then_inc(s_h0, 1)
            each_chunk(act, normalise)

            def stage_indices(layer):
                with act.Fori(0, ITERS) as i:
                    for h in range(2):
                        act.wait_ge(s_sum, i * 2 + (2 * ITERS * layer + h + 1))
                        nc.scalar.activation(idx_now[:, h, :], idx_all[:, ds(i * PER_IT + h * HALF, HALF)],
                                             ACT.Copy).then_inc(s_idx, 1)

            act.wait_ge(s_edges, 2)
            act.wait_ge(s_weights, 16 * 13)
            act.wait_ge(s_h0T, CHUNKS)
            stage_indices(0)

            def evacuate_z(n, u, t):
                act.wait_ge(s_zmm, n + 1)
                for m in range(2):
                    nc.scalar.activation(big[:, m, ds(n * CH, CH)], ps[:, u, m * CH:(m + 1) * CH], ACT.Identity,
                                         bias=cols[:, 0, m:m + 1]).then_inc(s_z, 1)
            each_chunk(act, evacuate_z)

            def batch_norm_sd(layer):
                act.wait_ge(s_bnvar, layer + 1)
                nc.scalar.activation(bn_tmp[:, :], bn_tmp[:, :], ACT.Sqrt).then_inc(s_bnsd, 1)
                act.wait_ge(s_bn, layer + 1)

            def relu_chunk(n, u, staged):
                for m in range(2):
                    nc.scalar.activation(h_stage[:, u, m, :], big[:, m, ds(n * CH, CH)], ACT.Relu,
                                         bias=bn_shift[:, m:m + 1], scale=bn_scale[:, m:m + 1]).then_inc(staged, 1)

            def evacuate_self(n, u, t):
                act.wait_ge(s_selfmm, n + 1)
                wait(act, s_self_out[u], t * 16)
                for m in range(2):
                    nc.scalar.activation(self_stage[:, u, m, :], ps[:, 4 + u, m * CH:(m + 1) * CH], ACT.Identity,
                                         bias=cols[:, 3, m:m + 1]).then_inc(s_selfev, 1)

            def relu_and_self(n, u, t):
                wait(act, s_selfmm, n - 1)
                relu_chunk(n, u, s_h)
                if not isinstance(n, int) or n > 0:
                    evacuate_self(n - 1, 1 - u, t if u else t - 1)

            batch_norm_sd(0)
            each_chunk(act, relu_and_self, peeled=2)
            evacuate_self(CHUNKS - 1, 0, CHUNKS // 2)
            stage_indices(1)

            def relu_2(n, u, t):
                wait(act, s_pmm, n - 1)
                relu_chunk(n, u, s_h2)
            batch_norm_sd(1)
            each_chunk(act, relu_2)
            act.wait_ge(s_pmm, CHUNKS)
            act.wait_ge(s_r2, CHUNKS)
            stage_indices(2)

        @block.tensor
        def _(pe):
            pe.sem_inc(s_sum, 2)

            pe.wait_ge(s_const, 7)
            pe.wait_ge(s_cmp, KCH)
            for c in range(KCH):
                last = nc.tensor.matmul(ps[:, 0, 0:BLOCKS - 1], ones[:, :], starts_below[:, c, :],
                                        start=(c == 0), stop=(c == KCH - 1))
            last.then_inc(s_counts, 1)

            pe.wait_ge(s_natf, KCH + 1)
            for k, nat in enumerate((src_f, rel_f)):
                for c in range(KCH):
                    last = nc.tensor.transpose(ps[:, 4 * k + c // 4, (c % 4) * P:(c % 4 + 1) * P],
                                               nat[:, c * P:(c + 1) * P], ident[:, :])
                last.then_inc(s_edgeT, 1)

            def transpose_h0(n, u, t):
                pe.wait_ge(s_h0, (n + 1) * 2)
                wait(pe, s_h0ev, n - 1)
                for j in range(2):
                    last = nc.tensor.transpose(ps[:, u, j * P:(j + 1) * P], h_stage[:, u, 0, j * P:(j + 1) * P],
                                               ident[:, :])
                last.then_inc(s_h0T, 1)
            pe.wait_ge(s_edges, 2)
            each_chunk(pe, transpose_h0)
            pe.wait_ge(s_h0ev, CHUNKS)

            def sum_edges(layer):
                with pe.Fori(0, ITERS) as i:
                    for h in range(2):
                        pe.wait_ge(s_hot, i * 2 + (2 * ITERS * layer + h + 1))
                        pe.wait_ge(s_rows[h], i * (16 * HALF) + 16 * HALF * (ITERS * layer + 1))
                        pe.wait_ge(s_acc, i * PER_IT + (PER_IT * ITERS * layer + HALF * (h + 1)))
                        for j in range(HALF):
                            k = h * HALF + j
                            step = ps[:, k // 2, (k % 2) * 256:(k % 2) * 256 + 256]
                            if layer == 2:
                                last = nc.tensor.matmul(step[:, 0:P], onehot[:, k, :], ring[:, k, 0:OUT_C],
                                                        start=True, stop=True)
                                continue
                            second = ones[:, :] if layer == 0 else ring[:, k, P:2 * P]
                            nc.tensor.matmul(step[:, 0:P], ring[:, k, 0:P], onehot[:, k, :], start=True, stop=True)
                            last = nc.tensor.matmul(step[:, P:2 * P], second, onehot[:, k, :], start=True, stop=True)
                        last.then_inc(s_sum, 1)

            sum_edges(0)

            pe.wait_ge(s_weights, 16 * 13)
            pe.wait_ge(s_acc, PER_IT + PER_IT * ITERS)

            def z_chunk(n, u, t):
                pe.wait_ge(s_mean, n + 1)
                wait(pe, s_z, (n - 1) * 2)
                for m in range(2):
                    zm = ps[:, u, m * CH:(m + 1) * CH]
                    nc.tensor.matmul(zm, w0[:, 0, m * P:(m + 1) * P], big[:, 1, ds(n * CH, CH)], start=True, stop=False)
                    last = nc.tensor.matmul(zm, w0[:, 1, m * P:(m + 1) * P], big[:, 0, ds(n * CH, CH)],
                                            start=False, stop=True)
                last.then_inc(s_zmm, 1)
            each_chunk(pe, z_chunk)
            pe.wait_ge(s_z, 2 * CHUNKS)

            def rows_and_self(n, u, t):
                pe.wait_ge(s_h, (n + 1) * 2)
                wait(pe, s_rowev, n - 1)
                for j in range(2):
                    for k in range(2):
                        last = nc.tensor.matmul(ps[:, u, j * HID:(j + 1) * HID], h_stage[:, u, k, j * P:(j + 1) * P],
                                                w1[:, 0, k, :], start=(k == 0), stop=(k == 1))
                last.then_inc(s_rowmm, 1)
                wait(pe, s_selfev, (n - 1) * 2)
                for m in range(2):
                    for k in range(2):
                        last = nc.tensor.matmul(ps[:, 4 + u, m * CH:(m + 1) * CH], w1[:, 1, k, m * P:(m + 1) * P],
                                                h_stage[:, u, k, :], start=(k == 0), stop=(k == 1))
                last.then_inc(s_selfmm, 1)
            each_chunk(pe, rows_and_self)
            pe.wait_ge(s_rowev, CHUNKS)
            pe.wait_ge(s_selfev, 2 * CHUNKS)
            sum_edges(1)

            pe.wait_ge(s_acc, PER_IT + 2 * PER_IT * ITERS)

            def rows_2(n, u, t):
                pe.wait_ge(s_h2, (n + 1) * 2)
                wait(pe, s_r2, n - 1)
                for j in range(2):
                    for k in range(2):
                        last = nc.tensor.matmul(ps[:, u, j * 2 * OUT_C:(j + 1) * 2 * OUT_C],
                                                h_stage[:, u, k, j * P:(j + 1) * P], w2[:, k, :],
                                                start=(k == 0), stop=(k == 1))
                last.then_inc(s_pmm, 1)
            each_chunk(pe, rows_2)
            pe.wait_ge(s_r2, CHUNKS)
            sum_edges(2)

        @block.vector
        def _(dve):
            V = nc.vector
            done = [0]

            def link(ins):
                done[0] += 1
                ins.then_inc(s_dve, 1)
                dve.wait_ge(s_dve, done[0])

            dve.sem_inc(s_acc, PER_IT)
            dve.wait_ge(s_const, 7)
            link(V.tensor_scalar(ident[:, :], iota_row[:, :], part_col[:, 0:1], None, ALU.is_equal))

            dve.wait_ge(s_firsts, 16)
            link(V.tensor_copy(firsts_f[:, :], firsts[:, :]))
            for c in range(KCH):
                V.tensor_scalar(starts_below[:, c, :], block_end[:, :], firsts_f[:, c:c + 1], None,
                                ALU.is_gt).then_inc(s_cmp, 1)
            dve.wait_ge(s_counts, 1)
            link(V.tensor_scalar(ends[:, :], ps[:, 0, 0:BLOCKS - 1], 1.0, None, ALU.max))
            link(V.tensor_tensor(ends[:, :], ends[:, :], block_no[:, :], ALU.add))
            for c in range(KCH):
                left = V.tensor_scalar(below[:, c, :], ends[:, :], step_no[:, c:c + 1], 0.0, ALU.is_le, ALU.add,
                                       accum_out=block_of[:, c:c + 1])
                if c == KCH - 1:
                    link(left)
            link(V.tensor_scalar(first_node[:, :], block_of[:, :], float(P), None, ALU.mult))
            V.tensor_copy(first_node_i[:, :], first_node[:, :])
            link(V.tensor_tensor(tile_no[:, :], step_no[:, :], block_of[:, :], ALU.subtract))
            dve.sem_inc(s_ids, 1)

            dve.wait_ge(s_x, 32)
            with dve.Fori(0, CHUNKS) as n:
                for j in range(2):
                    V.bn_stats(stats[:, ds(n * 2 + j, 1), :].rearrange("p a s -> p (a s)"),
                               x_nat[:, ds(n * 2 + j, 1), :].rearrange("p a f -> p (a f)")).then_inc(s_lnst, 1)
            dve.wait_ge(s_lnst, BLOCKS)
            half_diff = mv[:, :, 1]
            link(V.tensor_tensor(mv[:, :, 0], stats[:, :, 1], stats[:, :, 4], ALU.add))
            link(V.tensor_scalar(mv[:, :, 0], mv[:, :, 0], 0.5, None, ALU.mult))
            link(V.tensor_tensor(half_diff, mv[:, :, 0], stats[:, :, 4], ALU.subtract))
            link(V.tensor_tensor(half_diff, half_diff, half_diff, ALU.mult))
            link(V.tensor_tensor(rstd[:, :], stats[:, :, 2], stats[:, :, 5], ALU.add))
            link(V.scalar_tensor_tensor(out=rstd[:, :], in0=rstd[:, :], scalar=1.0 / IN_C, in1=half_diff,
                                        op0=ALU.mult, op1=ALU.add))
            V.tensor_scalar(rstd[:, :], rstd[:, :], EPS, None, ALU.add).then_inc(s_var, 1)
            dve.wait_ge(s_sd, 1)
            link(V.reciprocal(rstd[:, :], rstd[:, :]))
            V.scalar_tensor_tensor(out=nbias[:, :], in0=mv[:, :, 0], scalar=-1.0, in1=rstd[:, :],
                                   op0=ALU.mult, op1=ALU.mult).then_inc(s_lncoef, 1)

            dve.wait_ge(s_nat, 16 * 2 * KCH)
            V.tensor_copy(src_f, src_nat).then_inc(s_natf, 1)
            for c in range(KCH):
                V.tensor_scalar(rel_f[:, c * P:(c + 1) * P], dst_nat[:, c * P:(c + 1) * P], first_node[:, c:c + 1],
                                None, ALU.subtract).then_inc(s_natf, 1)
            flat_ps = ps[:, :, :].rearrange("p a b -> p (a b)")
            for k, to in enumerate((idx_all, rel_all)):
                dve.wait_ge(s_edgeT, k + 1)
                V.tensor_copy(to[:, :], flat_ps[:, k * 2048:k * 2048 + STEPS]).then_inc(s_edges, 1)

            def keep_h0T(n, u, t):
                dve.wait_ge(s_h0T, n + 1)
                V.tensor_copy(big[:, 0, ds(n * CH, CH)], ps[:, u, 0:CH]).then_inc(s_h0ev, 1)
            each_chunk(dve, keep_h0T)
            dve.wait_ge(s_brow, 16)
            dve.wait_ge(s_edges, 2)
            V.memset(big[:, 1:3, :], 0.0).then_inc(s_zero, 1)
            dve.wait_ge(s_zero, 1)

            def hot(layer, i, h, j):
                if j == 0:
                    dve.wait_ge(s_sum, i * 2 + (2 * ITERS * layer + h + 1))
                k = h * HALF + j
                ins = V.tensor_scalar(onehot[:, k, :], iota_row[:, :], rel_all[:, ds(i * PER_IT + k, 1)], None,
                                      ALU.is_equal)
                if j == HALF - 1:
                    ins.then_inc(s_hot, 1)

            def accumulate(layer, i, h, j, node):
                if j == 0:
                    dve.wait_ge(s_sum, i * 2 + (2 * ITERS * layer + h + 3))
                k = h * HALF + j
                dve.wait_ge(s_acc, i * PER_IT + (PER_IT * ITERS * layer + PER_IT + k))
                step = ps[:, k // 2, (k % 2) * 256:(k % 2) * 256 + 256]
                if layer == 2:
                    sums = big[:, 0, ds(node, P)]
                    V.tensor_tensor(sums, sums, step[:, 0:P], ALU.add).then_inc(s_acc, 1)
                else:
                    first = 1 if layer == 0 else 0
                    sums = big[:, first:first + 2, ds(node, P)]
                    V.tensor_tensor(sums, sums, step.rearrange("p (m c) -> p m c", m=2), ALU.add).then_inc(s_acc, 1)

            def nodes_of(i):
                _, values = nc.values_load_multi_w_load_instructions(
                    block_row[0:1, ds(i * PER_IT, PER_IT)], engines=[mybir.EngineType.DVE],
                    min_val=0, max_val=PADDED - P,
                    skip_runtime_bounds_check_because="the block of a step is a count of at most BLOCKS - 1 ends")
                return values

            def sum_edges(layer):
                for h in range(2):
                    for j in range(HALF):
                        hot(layer, 0, h, j)
                with dve.Fori(0, ITERS - 1) as i:
                    nodes = nodes_of(i)
                    for h in range(2):
                        for j in range(HALF):
                            accumulate(layer, i, h, j, nodes[h * HALF + j])
                            hot(layer, i + 1, h, j)
                nodes = nodes_of(ITERS - 1)
                for h in range(2):
                    for j in range(HALF):
                        accumulate(layer, ITERS - 1, h, j, nodes[h * HALF + j])
                dve.wait_ge(s_acc, PER_IT + PER_IT * ITERS * (layer + 1))

            sum_edges(0)

            link(V.tensor_scalar(big[:, 2, :], big[:, 2, :], 1.0, None, ALU.max))
            link(V.reciprocal(big[:, 2, :], big[:, 2, :]))
            dve.sem_inc(s_inv, 1)

            def mean(n, u, t):
                V.tensor_tensor(big[:, 1, ds(n * CH, CH)], big[:, 1, ds(n * CH, CH)], big[:, 2, ds(n * CH, CH)],
                                ALU.mult).then_inc(s_mean, 1)
            each_chunk(dve, mean)

            def chunk_stats(n):
                c = LAST_COLS if last_chunk(n) else CH
                for m in range(2):
                    V.bn_stats(stats[:, ds(n + m * CHUNKS, 1), :].rearrange("p a s -> p (a s)"),
                               big[:, m, ds(n * CH, c)]).then_inc(s_bnst, 1)

            def stats_z(n, u, t):
                dve.wait_ge(s_z, (n + 1) * 2)
                chunk_stats(n)
            each_chunk(dve, stats_z)

            def batch_norm(layer):
                dve.wait_ge(s_bnst, 2 * CHUNKS * (layer + 1))
                for m in range(2):
                    link(V.bn_aggr(bn_mv[:, m, :],
                                   stats[:, m * CHUNKS:(m + 1) * CHUNKS, :].rearrange("p a s -> p (a s)")))
                V.tensor_scalar(bn_tmp[:, :], bn_mv[:, :, 1], EPS, None, ALU.add).then_inc(s_bnvar, 1)
                dve.wait_ge(s_bnsd, layer + 1)
                link(V.reciprocal(bn_tmp[:, :], bn_tmp[:, :]))
                link(V.tensor_tensor(bn_scale[:, :], bn_tmp[:, :], cols[:, 3 * layer + 1, :], ALU.mult))
                link(V.tensor_tensor(bn_tmp[:, :], bn_mv[:, :, 0], bn_scale[:, :], ALU.mult))
                V.tensor_tensor(bn_shift[:, :], cols[:, 3 * layer + 2, :], bn_tmp[:, :], ALU.subtract).then_inc(s_bn, 1)
            dve.wait_ge(s_weights, 16 * 13)
            batch_norm(0)

            def keep_rows_1(n, u, t):
                dve.wait_ge(s_rowmm, n + 1)
                wait(dve, s_row_out[u], t * 16)
                V.tensor_copy(row_stage[:, u].rearrange("p j c -> p (j c)"), ps[:, u, :]).then_inc(s_rowev, 1)
                V.tensor_copy(big[:, 0:2, ds(n * CH, CH)], zeros[:, :, :].to_broadcast([P, 2, CH])).then_inc(s_zero, 1)
            each_chunk(dve, keep_rows_1)
            dve.wait_ge(s_zero, 1 + CHUNKS)
            sum_edges(1)

            for m in range(2):
                link(V.tensor_tensor(big[:, m, :], big[:, m, :], big[:, 2, :], ALU.mult))

            def add_self(n, u, t):
                dve.wait_ge(s_self_in[u], t * 16 + 16)
                for m in range(2):
                    V.tensor_tensor(big[:, m, ds(n * CH, CH)], big[:, m, ds(n * CH, CH)], self_stage[:, u, m, :],
                                    ALU.add).then_inc(s_zadd, 1)
                if not isinstance(n, int) or n > 0:
                    dve.wait_ge(s_zadd, n * 2)
                    chunk_stats(n - 1)
            each_chunk(dve, add_self)
            dve.wait_ge(s_zadd, 2 * CHUNKS)
            chunk_stats(CHUNKS - 1)
            batch_norm(1)

            def keep_rows_2(n, u, t):
                dve.wait_ge(s_x2[u], 16 * t + (32 if last_chunk(n) else 16))
                xs = row_stage[:, u, 1, :].rearrange("p (j f) -> p j f", j=2)
                V.tensor_tensor(xs, xs, bl2_all[:, :].rearrange("p (a f) -> p a f", a=1).to_broadcast([P, 2, OUT_C]),
                                ALU.add).then_inc(s_x2b, 1)
                dve.wait_ge(s_pmm, n + 1)
                wait(dve, s_p_out[u], t * 16)
                both = ps[:, u, :].rearrange("p (j c) -> p j c", j=2)
                V.tensor_copy(row_stage[:, u, 0, :].rearrange("p (j f) -> p j f", j=2),
                              both[:, :, 0:OUT_C]).then_inc(s_pev, 1)
                dve.wait_ge(s_x2b, n + 1)
                V.tensor_tensor(res[:, ds(n * 2, 2), :], both[:, :, OUT_C:2 * OUT_C], xs, ALU.add).then_inc(s_r2, 1)
                V.tensor_copy(big[:, 0, ds(n * CH, CH)], zeros[:, 0, :]).then_inc(s_zero, 1)
            each_chunk(dve, keep_rows_2)
            dve.wait_ge(s_zero, 1 + 2 * CHUNKS)
            dve.wait_ge(s_r2, CHUNKS)
            sum_edges(2)

            dve.wait_ge(s_inv_col, 16)

            def finish(n, u, t):
                for j in range(2):
                    b = n * 2 + j
                    r = res[:, ds(b, 1), :].rearrange("p a f -> p (a f)")
                    V.scalar_tensor_tensor(out=r, in0=big[:, 0, ds(b * P, P)], scalar=inv_col[:, ds(b, 1)], in1=r,
                                           op0=ALU.mult, op1=ALU.add).then_inc(s_fin, 1)
            each_chunk(dve, finish)


_INS = ["x", "src", "dst", "L0_gnn_Wl0", "L0_gnn_bl0", "L0_gnn_Wr0", "L0_gnn_g0", "L0_gnn_b0", "L0_gnn_Wl1",
        "L0_gnn_bl1", "L0_gnn_Wr1", "L0_gnn_g1", "L0_gnn_b1", "L0_gnn_Wl2", "L0_gnn_bl2", "L0_gnn_Wr2"]


def kernel(**inputs):
    import numpy as _np
    import concourse.bacc as _bacc
    from concourse import mybir as _mybir
    from concourse.bass_utils import run_bass_kernel_spmd as _run

    nc = _bacc.Bacc("TRN2", target_bir_lowering=False, num_devices=1)
    arrays, args = {}, []
    for name in _INS:
        a = _np.ascontiguousarray(inputs[name])
        arrays[f"in_{name}"] = a
        args.append(nc.dram_tensor(f"in_{name}", a.shape, _mybir.dt.from_np(a.dtype), kind="ExternalInput").ap())
    args.append(nc.dram_tensor("out_0", (NODES, OUT_C), _mybir.dt.float32, kind="ExternalOutput").ap())
    gnn_kernel(nc, *args)
    r = _run(nc, [arrays], core_ids=[0])
    return r.results[0]["out_0"]
```

```python
import concourse.bass as bass
from concourse import mybir
from contextlib import ExitStack

P = 128
NODES = 12500
EDGES = 200000
IN_C, HID, OUT_C = 128, 256, 128
EPS = 1e-5

BLOCKS = -(-NODES // P)
PADDED = BLOCKS * P
LAST_ROWS = NODES - (BLOCKS - 1) * P
TILES = -(-EDGES // P)
WALK = TILES + BLOCKS - 1
KCH = -(-WALK // P)
STEPS = KCH * P
HALF = 8
PER_IT = 2 * HALF
PART = HALF // 2
ITERS = -(-TILES // PER_IT)
MAIN = ITERS * PER_IT
LATE = STEPS - MAIN
FULL_C = TILES // P
FULL_TILES = EDGES // P - FULL_C * P
LEFT = EDGES % P
TAB_ROWS = STEPS
PAD_EDGES = TAB_ROWS * P - EDGES
BUCKETS = BLOCKS + 1
NO_NODE = 1 << 20
CH = 2 * P
CHUNKS = PADDED // CH
DEPTH = 4
WIDE = 8
GROUPS = 3
OUT_PARTS = 7
LAST_COLS = NODES - (CHUNKS - 1) * CH


def gnn_kernel(nc, x, src, dst, Wl0, bl0, Wr0, g0, b0, Wl1, bl1, Wr1, g1, b1, Wl2, bl2, Wr2, out):
    f32 = mybir.dt.float32
    i32 = mybir.dt.int32
    u32 = mybir.dt.uint32
    ALU = mybir.AluOpType
    ACT = mybir.ActivationFunctionType
    ds = bass.ds

    ctx = ExitStack()
    with ctx:
        def sb(name, shape, dt=f32):
            return ctx.enter_context(nc.sbuf_tensor(name, shape, dt))

        def sem(name):
            return ctx.enter_context(nc.semaphore(name))

        def dram(name, shape, dt=f32):
            return nc.dram_tensor(name, shape, dt, kind="Internal").ap()

        src_tab = dram("src_tab", [TAB_ROWS, P], i32)
        dst_tab = dram("dst_tab", [TAB_ROWS, P], i32)
        node_dram = dram("node_dram", [STEPS], i32)
        degree_dram = dram("degree_dram", [PADDED])
        inverse_dram = dram("inverse_dram", [PADDED])
        table = [dram("table0", [PADDED, IN_C]), dram("table1", [PADDED, HID]), dram("table2", [PADDED, OUT_C])]

        big = sb("big", [P, 3, PADDED])
        ring = sb("ring", [P, PER_IT, HID])
        onehot = sb("onehot", [P, PER_IT, P])
        idx_all = sb("idx_all", [P, STEPS], i32)
        rel_all = sb("rel_all", [P, STEPS])
        node_row = sb("node_row", [1, STEPS], i32)
        idx_now = sb("idx_now", [P, 2, HALF], i32)
        w0 = sb("w0", [P, 2, HID])
        w1 = sb("w1", [P, 2, 2, HID])
        w2 = sb("w2", [P, 2, 2 * OUT_C])
        cols = sb("cols", [P, 6, 2])
        bl2_col = sb("bl2_col", [P, 1])
        iota_row = sb("iota_row", [P, P])
        part_col = sb("part_col", [P, 1])
        ident = sb("ident", [P, P])
        ones = sb("ones", [P, P])
        block_end = sb("block_end", [P, BLOCKS - 1])
        block_no = sb("block_no", [P, BLOCKS - 1])
        step_no = sb("step_no", [P, KCH])
        pads = sb("pads", [P, 2, P], i32)
        degrees = sb("degrees", [P, BLOCKS])
        firsts = sb("firsts", [P, KCH], i32)
        firsts_f = sb("firsts_f", [P, KCH])
        ends = sb("ends", [P, BLOCKS - 1])
        block_of = sb("block_of", [P, KCH])
        first_node = sb("first_node", [P, KCH])
        first_node_i = sb("first_node_i", [P, KCH], i32)
        tile_no = sb("tile_no", [P, KCH], i32)
        stats = sb("stats", [P, 2 * CHUNKS, 6])
        rstd = sb("rstd", [P, BLOCKS])
        bn_mv = sb("bn_mv", [P, 2, 2])
        bn_scale = sb("bn_scale", [P, 2])
        bn_shift = sb("bn_shift", [P, 2])
        bn_tmp = sb("bn_tmp", [P, 2])
        outside = sb("outside", [P, 1], i32)

        row_stage = ring[:, 0:2 * DEPTH, :].rearrange("p (u j) c -> p u j c", u=DEPTH)
        h0_stage = ring[:, 2 * DEPTH:4 * DEPTH, :]
        h_stage = ring[:, 2 * DEPTH:4 * DEPTH, :].rearrange("p (u j) c -> p u j c", u=DEPTH)
        src_nat = big[:, 2, 0:STEPS].bitcast(i32)
        dst_nat = big[:, 2, STEPS:2 * STEPS].bitcast(i32)
        src_f = big[:, 2, 2 * STEPS:3 * STEPS]
        rel_f = big[:, 2, 3 * STEPS:4 * STEPS]
        starts_below = big[:, 2, 4 * STEPS:4 * STEPS + KCH * (BLOCKS - 1)].rearrange("p (c b) -> p c b", c=KCH)
        below = big[:, 2, 6 * STEPS:6 * STEPS + KCH * (BLOCKS - 1)].rearrange("p (c b) -> p c b", c=KCH)
        inside = big[:, 2, 4 * STEPS:5 * STEPS]
        src_by_edge, dst_by_edge = (big[:, 0, k * STEPS:(k + 1) * STEPS].bitcast(i32) for k in range(2, 4))
        bucket_i = big[:, 0, 4 * STEPS:5 * STEPS].bitcast(i32)
        bucket = big[:, 0, 5 * STEPS:6 * STEPS]
        sort_area = big[:, 0, 6 * STEPS:6 * STEPS + 8 * P].rearrange("p (k n) -> p k n", n=P)
        in_bucket, counts, base, before, earlier, bucket_no = (sort_area[:, k, 0:BUCKETS] for k in range(6))
        is_before = sort_area[:, 6, :]
        inside_sum, place = sort_area[:, 7, 0:1], sort_area[:, 7, 1:2]
        place_i = sort_area[:, 7, 2:3].bitcast(i32)
        moved = sort_area[:, 7, 3:5].bitcast(i32)

        ln_area = ring[:, 0:2, :].rearrange("p a c -> p (a c)")
        mv = ln_area[:, 0:2 * BLOCKS].rearrange("p (b s) -> p b s", s=2)
        nbias = ln_area[:, 2 * BLOCKS:3 * BLOCKS]
        x_nat = big[:, 1, :].rearrange("p (b f) -> p b f", f=IN_C)

        ps = ctx.enter_context(nc.psum_tensor("ps", [P, 8, 512], f32))

        s_const = sem("s_const")
        s_pads = sem("s_pads")
        s_weights = sem("s_weights")
        s_dst = sem("s_dst")
        s_src = sem("s_src")
        s_x = [sem(f"s_x{g}") for g in range(GROUPS)]
        s_insides = sem("s_insides")
        s_total = sem("s_total")
        s_outside = sem("s_outside")
        s_tabs = sem("s_tabs")
        s_by_edge = sem("s_by_edge")
        s_onehot = sem("s_onehot")
        s_tally = sem("s_tally")
        s_tallied = sem("s_tallied")
        s_place = sem("s_place")
        s_begin = sem("s_begin")
        s_moved = sem("s_moved")
        s_order = sem("s_order")
        s_firsts = sem("s_firsts")
        s_cmp = sem("s_cmp")
        s_counts = sem("s_counts")
        s_ids = sem("s_ids")
        s_nat = sem("s_nat")
        s_windows = sem("s_windows")
        s_row_made = sem("s_row_made")
        s_node_row = sem("s_node_row")
        s_natf = sem("s_natf")
        s_edgeT = sem("s_edgeT")
        s_edges = sem("s_edges")
        s_dve = sem("s_dve")
        s_sort = sem("s_sort")
        s_lnst = sem("s_lnst")
        s_var = sem("s_var")
        s_sd = sem("s_sd")
        s_lncoef = sem("s_lncoef")
        s_h0 = sem("s_h0")
        s_h0T = sem("s_h0T")
        s_h0ev = sem("s_h0ev")
        s_h0_out = [sem(f"s_h0_out{u}") for u in range(WIDE)]
        s_tables = sem("s_tables")
        s_zero = sem("s_zero")
        s_idx = sem("s_idx")
        s_half = sem("s_half")
        s_rows = [sem(f"s_rows{k}") for k in range(PER_IT // PART)]
        s_hot = sem("s_hot")
        s_sum = sem("s_sum")
        s_acc = sem("s_acc")
        s_late_idx = sem("s_late_idx")
        s_late_begin = sem("s_late_begin")
        s_late_rows = sem("s_late_rows")
        s_late_hot = sem("s_late_hot")
        s_late_sum = sem("s_late_sum")
        s_late_acc = sem("s_late_acc")
        s_summed = sem("s_summed")
        s_degree_out = sem("s_degree_out")
        s_degree = sem("s_degree")
        s_inv = sem("s_inv")
        s_inv_out = sem("s_inv_out")
        s_inv_all = [sem(f"s_inv_all{g}") for g in range(GROUPS)]
        s_mean = sem("s_mean")
        s_zmm = sem("s_zmm")
        s_z = sem("s_z")
        s_bnst = sem("s_bnst")
        s_bnvar = sem("s_bnvar")
        s_bnsd = sem("s_bnsd")
        s_bn = sem("s_bn")
        s_h = sem("s_h")
        s_rowmm = sem("s_rowmm")
        s_selfmm = sem("s_selfmm")
        s_rowev = sem("s_rowev")
        s_selfev = sem("s_selfev")
        s_row_out = [sem(f"s_row_out{u}") for u in range(DEPTH)]
        s_h2 = sem("s_h2")
        s_pmm = sem("s_pmm")
        s_pev = sem("s_pev")
        s_self2 = sem("s_self2")
        s_p_out = [sem(f"s_p_out{u}") for u in range(DEPTH)]
        s_x_again = sem("s_x_again")
        s_fin = sem("s_fin")
        s_finT = sem("s_finT")
        s_res = sem("s_res")
        s_out = sem("s_out")

        def chunks_of(u, depth=DEPTH):
            return CHUNKS // depth + (1 if u < CHUNKS % depth else 0)

        def each_chunk(eng, body, depth=DEPTH, before=None):
            turns = CHUNKS // depth
            for g in range(GROUPS if before else 1):
                first, last = (g * turns // GROUPS, (g + 1) * turns // GROUPS) if before else (0, turns)
                if before:
                    before(g)
                if g == 0:
                    for u in range(depth):
                        body(u, u, 0)
                with eng.Fori(max(first, 1), last) as t:
                    for u in range(depth):
                        body(t * depth + u, u, t)
            body(CHUNKS - 1, 0, turns)

        def group(g):
            turns = CHUNKS // WIDE
            return g * turns // GROUPS * WIDE, CHUNKS if g == GROUPS - 1 else (g + 1) * turns // GROUPS * WIDE

        def wait(eng, s, value):
            if not isinstance(value, int) or value > 0:
                eng.wait_ge(s, value)

        def last_chunk(n):
            return isinstance(n, int) and n == CHUNKS - 1

        def if_irregular(eng):
            eng.wait_ge(s_outside, 1)
            return eng.If(nc.values_load(outside[0:1, 0:1], engines=[eng.engine], min_val=0, max_val=STEPS * P) > 0)

        block = ctx.enter_context(nc.Block())

        @block.sync
        def _(sp):
            sp.wait_ge(s_pads, 5)
            cols_end = FULL_C * P * P
            for edges, nat, loaded in ((dst, dst_nat, s_dst), (src, src_nat, s_src)):
                sp.dma_start(nat[:, 0:FULL_C * P].rearrange("p (c e) -> p c e", e=P),
                             edges[0:cols_end].rearrange("(c p e) -> p c e", p=P, e=P)).then_inc(loaded, 16)
                sp.dma_start(nat[0:FULL_TILES, FULL_C * P:(FULL_C + 1) * P],
                             edges[cols_end:cols_end + FULL_TILES * P].rearrange("(p e) -> p e", e=P)).then_inc(loaded, 16)
                sp.dma_start(nat[FULL_TILES:FULL_TILES + 1, FULL_C * P:FULL_C * P + LEFT],
                             edges[EDGES - LEFT:EDGES].rearrange("(a n) -> a n", a=1)).then_inc(loaded, 16)
            for g in range(GROUPS):
                first, end = (2 * n for n in group(g))
                full = min(end, BLOCKS - 1)
                sp.dma_start(x_nat[:, first:full, :],
                             x[first * P:full * P, :].rearrange("(b p) f -> p b f", p=P)).then_inc(s_x[g], 16)
            sp.dma_start(x_nat[0:LAST_ROWS, BLOCKS - 1, :], x[(BLOCKS - 1) * P:NODES, :]).then_inc(s_x[GROUPS - 1], 16)

            with if_irregular(sp):
                flat = [tab.rearrange("t e -> (t e)") for tab in (src_tab, dst_tab)]
                full = PAD_EDGES // P
                left = PAD_EDGES - full * P
                for k, (tab, edges) in enumerate(zip(flat, (src, dst))):
                    sp.dma_start(tab[0:EDGES].rearrange("(a n) -> a n", a=16),
                                 edges.rearrange("(a n) -> a n", a=16)).then_inc(s_tabs, 16)
                    sp.dma_start(tab[EDGES:EDGES + full * P].rearrange("(a n) -> a n", n=P),
                                 pads[0:full, k, :]).then_inc(s_tabs, 16)
                    sp.dma_start(tab[EDGES + full * P:EDGES + full * P + left].rearrange("(a n) -> a n", a=1),
                                 pads[0:1, k, 0:left]).then_inc(s_tabs, 16)
                sp.wait_ge(s_tabs, 16 * 6)
                with nc.allow_non_contiguous_dma(reason="only for edges that come unsorted"):
                    for tab, to in ((src_tab, src_by_edge), (dst_tab, dst_by_edge)):
                        sp.dma_start(to, tab[0:TAB_ROWS, :].rearrange("t e -> e t")).then_inc(s_by_edge, 16)
                sp.wait_ge(s_order, 1)
                with nc.allow_non_contiguous_dma(reason="one word of each tile"):
                    sp.dma_start(firsts[:, :], dst_tab[0:TAB_ROWS, 0].rearrange("(c p) -> p c", p=P)).then_inc(s_firsts, 16)

            sp.wait_ge(s_windows, 1)
            with nc.allow_non_contiguous_dma(reason="one word a step"):
                sp.dma_start(node_dram.rearrange("(c p) -> p c", p=P), first_node_i[:, :]).then_inc(s_row_made, 16)
            sp.wait_ge(s_row_made, 16)
            sp.dma_start(node_row[0:1, :], node_dram.rearrange("(a n) -> a n", a=1)).then_inc(s_node_row, 16)

            tb0 = table[0].rearrange("(b p) f -> p b f", p=P)

            def store_h0(n, u, t):
                sp.wait_ge(s_h0, (n + 1) * 2)
                sp.dma_start(tb0[:, ds(n * 2, 2), :],
                             h0_stage[:, u, :].rearrange("p (j f) -> p j f", j=2)).then_inc(s_h0_out[u], 16)
            each_chunk(sp, store_h0, WIDE)
            for u in range(WIDE):
                sp.wait_ge(s_h0_out[u], 16 * chunks_of(u, WIDE))
            sp.sem_inc(s_tables, 1)

            sp.wait_ge(s_summed, 1)
            sp.dma_start(degree_dram.rearrange("(a n) -> a n", a=1), big[0:1, 2, :]).then_inc(s_degree_out, 16)
            sp.wait_ge(s_degree_out, 16)
            sp.dma_start(degrees[:, :], degree_dram.rearrange("(p j) -> p j", j=BLOCKS)).then_inc(s_degree, 16)
            sp.wait_ge(s_inv, 1)
            sp.dma_start(inverse_dram.rearrange("(p j) -> p j", j=BLOCKS), degrees[:, :]).then_inc(s_inv_out, 16)
            sp.wait_ge(s_inv_out, 16)
            for g in range(GROUPS):
                first, end = (CH * n for n in group(g))
                sp.dma_start(big[:, 2, first:end],
                             inverse_dram[first:end].rearrange("(a n) -> a n", a=1).to_broadcast([P, end - first])
                             ).then_inc(s_inv_all[g], 16)

            tb1 = table[1].rearrange("(b p) f -> p b f", p=P)

            def store_1(n, u, t):
                sp.wait_ge(s_rowev, n + 1)
                sp.dma_start(tb1[:, ds(n * 2, 2), :], row_stage[:, u]).then_inc(s_row_out[u], 16)
            each_chunk(sp, store_1)
            for u in range(DEPTH):
                sp.wait_ge(s_row_out[u], 16 * chunks_of(u))
            sp.sem_inc(s_tables, 1)

            tb2 = table[2].rearrange("(b p) f -> p b f", p=P)

            def store_2(n, u, t):
                sp.wait_ge(s_pev, n + 1)
                sp.dma_start(tb2[:, ds(n * 2, 2), :],
                             row_stage[:, u, 0, :].rearrange("p (j f) -> p j f", j=2)).then_inc(s_p_out[u], 16)
            each_chunk(sp, store_2)
            for u in range(DEPTH):
                sp.wait_ge(s_p_out[u], 16 * chunks_of(u))
            sp.sem_inc(s_tables, 1)

            body_rows = (BLOCKS - 1) * P
            for part in range(OUT_PARTS):
                sp.wait_ge(s_sum, 2 + 2 * (2 * ITERS + 2 * (part + 1)))
                first, end = (b * BLOCKS // OUT_PARTS for b in (part, part + 1))
                full = min(end, BLOCKS - 1)
                sp.dma_start(x_nat[:, first:full, :],
                             x[first * P:full * P, :].rearrange("(b p) f -> p b f", p=P)).then_inc(s_x_again, 16)
            sp.dma_start(x_nat[0:LAST_ROWS, BLOCKS - 1, :], x[body_rows:NODES, :]).then_inc(s_x_again, 16)

            for part in range(OUT_PARTS):
                first, end = (b * BLOCKS // OUT_PARTS for b in (part, part + 1))
                sp.wait_ge(s_res, end // 2)
                full = min(end, BLOCKS - 1)
                sp.dma_start(out[first * P:full * P, :].rearrange("(b p) f -> p b f", p=P),
                             x_nat[:, first:full, :]).then_inc(s_out, 16)
            sp.dma_start(out[body_rows:NODES, :], x_nat[0:LAST_ROWS, BLOCKS - 1, :]).then_inc(s_out, 16)
            sp.wait_ge(s_out, 16 * (OUT_PARTS + 1))

        @block.gpsimd
        def _(pool):
            pool.memset(pads[:, 0, :], 0).then_inc(s_pads, 1)
            pool.memset(pads[:, 1, :], NO_NODE).then_inc(s_pads, 1)
            pool.memset(dst_nat[:, FULL_C * P:(FULL_C + 1) * P], NO_NODE).then_inc(s_pads, 1)
            pool.memset(src_nat[:, FULL_C * P:(FULL_C + 1) * P], 0).then_inc(s_pads, 1)
            pool.memset(x_nat[:, BLOCKS - 1, :], 0.0).then_inc(s_pads, 1)
            f = dict(allow_small_or_imprecise_dtypes=True)
            pool.iota(iota_row[:, :], [[1, P]], base=0, channel_multiplier=0, **f).then_inc(s_const, 1)
            pool.iota(part_col[:, :], [[0, 1]], base=0, channel_multiplier=1, **f).then_inc(s_const, 1)
            pool.iota(block_end[:, :], [[P, BLOCKS - 1]], base=P, channel_multiplier=0, **f).then_inc(s_const, 1)
            pool.iota(block_no[:, :], [[1, BLOCKS - 1]], base=0, channel_multiplier=0, **f).then_inc(s_const, 1)
            pool.iota(step_no[:, :], [[P, KCH]], base=0, channel_multiplier=1, **f).then_inc(s_const, 1)
            pool.memset(ones[:, :], 1.0).then_inc(s_const, 1)

            with if_irregular(pool):
                with pool.Fori(0, TAB_ROWS) as t:
                    pool.wait_ge(s_place, t + 1)
                    pool.sem_inc(s_begin, 1)
                    for k, tab in enumerate((src_tab, dst_tab)):
                        pool.indirect_dma_start(
                            out=tab[0:TAB_ROWS, :].rearrange("t (e a) -> (t e) a", a=1),
                            out_offset=bass.IndirectOffsetOnAxis(ap=place_i.bitcast(u32), axis=0),
                            in_=moved[:, k:k + 1], in_offset=None).then_inc(s_moved, 16)
                    pool.wait_ge(s_moved, t * 32 + 32)
                pool.sem_inc(s_order, 1)
                pool.wait_ge(s_ids, 1)
                for c in range(KCH):
                    for tab, nat in ((src_tab, src_nat), (dst_tab, dst_nat)):
                        pool.indirect_dma_start(
                            out=nat[:, c * P:(c + 1) * P], out_offset=None, in_=tab[:, :],
                            in_offset=bass.IndirectOffsetOnAxis(ap=tile_no[:, c:c + 1].bitcast(u32), axis=0),
                        ).then_inc(s_nat, 16)

            pool.wait_ge(s_edges, 2)
            pool.memset(big[:, 2, :], 0.0).then_inc(s_zero, 1)

            for layer in range(3):
                width = table[layer].shape[1]
                pool.wait_ge(s_tables, layer + 1)
                with pool.Fori(0, ITERS) as i:
                    for h in range(2):
                        pool.wait_ge(s_idx, i * 2 + (2 * ITERS * layer + h + 1))
                        pool.sem_inc(s_half, 1)
                        for j in range(HALF):
                            pool.indirect_dma_start(
                                out=ring[:, h * HALF + j, 0:width], out_offset=None, in_=table[layer][:, :],
                                in_offset=bass.IndirectOffsetOnAxis(ap=idx_now[:, h, j:j + 1].bitcast(u32), axis=0),
                            ).then_inc(s_rows[(h * HALF + j) // PART], 16)
                with if_irregular(pool):
                    with pool.Fori(LATE * layer, LATE * (layer + 1)) as t:
                        pool.wait_ge(s_late_idx, t + 1)
                        pool.sem_inc(s_late_begin, 1)
                        pool.indirect_dma_start(
                            out=ring[:, 0, 0:width], out_offset=None, in_=table[layer][:, :],
                            in_offset=bass.IndirectOffsetOnAxis(ap=idx_now[:, 0, 0:1].bitcast(u32), axis=0),
                        ).then_inc(s_late_rows, 16)

        @block.scalar
        def _(act):
            for k, w in enumerate((Wl0, Wr0)):
                act.dma_start(w0[:, k, :], w).then_inc(s_weights, 16)
            for k, w in enumerate((Wl1, Wr1)):
                act.dma_start(w1[:, k], w.rearrange("(k p) n -> p k n", p=P)).then_inc(s_weights, 16)
            for k, w in enumerate((Wl2, Wr2)):
                act.dma_start(w2[:, :, k * OUT_C:(k + 1) * OUT_C],
                              w.rearrange("(k p) n -> p k n", p=P)).then_inc(s_weights, 16)
            with nc.allow_non_contiguous_dma(reason="vectors over the features"):
                for k, v in enumerate((bl0, g0, b0, bl1, g1, b1)):
                    act.dma_start(cols[:, k, :], v.rearrange("(m p) -> p m", p=P)).then_inc(s_weights, 16)
                act.dma_start(bl2_col[:, :], bl2.rearrange("(p a) -> p a", a=1)).then_inc(s_weights, 16)

            def group_sd(g):
                first, end = (2 * n for n in group(g))
                act.wait_ge(s_var, g + 1)
                nc.scalar.activation(rstd[:, first:end], rstd[:, first:end], ACT.Sqrt).then_inc(s_sd, 1)
                act.wait_ge(s_lncoef, g + 1)

            def normalise(n, u, t):
                wait(act, s_h0T, n - (WIDE - 1))
                wait(act, s_h0_out[u], t * 16)
                blocks, biases, scales = (a[:, ds(n * 2, 2)] for a in (x_nat, nbias, rstd))
                for j in range(2):
                    nc.scalar.activation(h0_stage[:, u, j * P:(j + 1) * P], blocks[:, j, :], ACT.Relu,
                                         bias=biases[:, j:j + 1], scale=scales[:, j:j + 1]).then_inc(s_h0, 1)
            each_chunk(act, normalise, WIDE, before=group_sd)
            act.wait_ge(s_h0T, CHUNKS)

            def stage_indices(layer):
                with act.Fori(0, ITERS) as i:
                    for h in range(2):
                        act.wait_ge(s_sum, i * 2 + (2 * ITERS * layer + h + 1))
                        nc.scalar.activation(idx_now[:, h, :], idx_all[:, ds(i * PER_IT + h * HALF, HALF)],
                                             ACT.Copy).then_inc(s_idx, 1)

            act.wait_ge(s_weights, 16 * 13)
            stage_indices(0)

            def evacuate_z(n, u, t):
                act.wait_ge(s_zmm, n + 1)
                z = big[:, 0:2, ds(n * CH, CH)]
                for m in range(2):
                    nc.scalar.activation(z[:, m, :], ps[:, u, m * CH:(m + 1) * CH], ACT.Identity,
                                         bias=cols[:, 0, m:m + 1]).then_inc(s_z, 1)
            each_chunk(act, evacuate_z, WIDE)

            def batch_norm_sd(layer):
                act.wait_ge(s_bnvar, layer + 1)
                nc.scalar.activation(bn_tmp[:, :], bn_tmp[:, :], ACT.Sqrt).then_inc(s_bnsd, 1)
                act.wait_ge(s_bn, layer + 1)

            def relu_chunk(n, u, staged):
                z = big[:, 0:2, ds(n * CH, CH)]
                for m in range(2):
                    nc.scalar.activation(h_stage[:, u, m, :], z[:, m, :], ACT.Relu,
                                         bias=bn_shift[:, m:m + 1], scale=bn_scale[:, m:m + 1]).then_inc(staged, 1)

            def relu_1(n, u, t):
                wait(act, s_selfmm, n - (DEPTH - 1))
                relu_chunk(n, u, s_h)

            batch_norm_sd(0)
            each_chunk(act, relu_1)
            act.wait_ge(s_selfmm, CHUNKS)
            stage_indices(1)

            def relu_2(n, u, t):
                wait(act, s_pmm, n - (DEPTH - 1))
                relu_chunk(n, u, s_h2)
            batch_norm_sd(1)
            each_chunk(act, relu_2)
            act.wait_ge(s_pmm, CHUNKS)
            stage_indices(2)

            act.wait_ge(s_summed, 3)

            def stage_result(n, u, t):
                wait(act, s_finT, n - (DEPTH - 1))
                nc.scalar.activation(h_stage[:, u, 0, :], big[:, 0, ds(n * CH, CH)], ACT.Copy).then_inc(s_fin, 1)
            each_chunk(act, stage_result)

        @block.tensor
        def _(pe):
            pe.sem_inc(s_sum, 2)

            pe.wait_ge(s_const, 6)
            pe.wait_ge(s_insides, 1)
            nc.tensor.matmul(ps[:, 0, 0:1], ones[:, :], inside_sum, start=True, stop=True).then_inc(s_total, 1)
            with if_irregular(pe):
                with pe.Fori(0, TAB_ROWS) as t:
                    pe.wait_ge(s_onehot, t + 1)
                    nc.tensor.matmul(ps[:, 0, 0:BUCKETS], ones[:, :], in_bucket, start=True, stop=True).then_inc(s_tally, 1)
                with pe.Fori(TAB_ROWS, 2 * TAB_ROWS) as t:
                    pe.wait_ge(s_onehot, t + 1)
                    nc.tensor.matmul(ps[:, 0, 0:BUCKETS], ones[:, :], in_bucket, start=True, stop=True)
                    nc.tensor.matmul(ps[:, 1, 0:BUCKETS], is_before, in_bucket, start=True, stop=True).then_inc(s_tally, 1)

                pe.wait_ge(s_cmp, KCH)
                for c in range(KCH):
                    last = nc.tensor.matmul(ps[:, 0, 0:BLOCKS - 1], ones[:, :], starts_below[:, c, :],
                                            start=(c == 0), stop=(c == KCH - 1))
                last.then_inc(s_counts, 1)

            pe.wait_ge(s_natf, 1)
            pe.wait_ge(s_outside, 1)
            for k, nat in enumerate((src_f, rel_f)):
                for c in range(KCH):
                    last = nc.tensor.transpose(ps[:, 4 * k + c // 4, (c % 4) * P:(c % 4 + 1) * P],
                                               nat[:, c * P:(c + 1) * P], ident[:, :])
                last.then_inc(s_edgeT, 1)

            def transpose_h0(n, u, t):
                pe.wait_ge(s_h0, (n + 1) * 2)
                wait(pe, s_h0ev, n - (WIDE - 1))
                for j in range(2):
                    last = nc.tensor.transpose(ps[:, u, j * P:(j + 1) * P], h0_stage[:, u, j * P:(j + 1) * P],
                                               ident[:, :])
                last.then_inc(s_h0T, 1)
            pe.wait_ge(s_edges, 2)
            each_chunk(pe, transpose_h0, WIDE)
            pe.wait_ge(s_h0ev, CHUNKS)

            def sum_edges(layer):
                with pe.Fori(0, ITERS) as i:
                    for h in range(2):
                        pe.wait_ge(s_hot, i * 2 + (2 * ITERS * layer + h + 1))
                        pe.wait_ge(s_acc, i * PER_IT + (PER_IT * ITERS * layer + HALF * (h + 1)))
                        for j in range(HALF):
                            k = h * HALF + j
                            if k % PART == 0:
                                pe.wait_ge(s_rows[k // PART], i * (16 * PART) + 16 * PART * (ITERS * layer + 1))
                            step = ps[:, k // 2, (k % 2) * 256:(k % 2) * 256 + 256]
                            if layer == 2:
                                last = nc.tensor.matmul(step[:, 0:P], ring[:, k, 0:OUT_C], onehot[:, k, :],
                                                        start=True, stop=True)
                                continue
                            second = ones[:, :] if layer == 0 else ring[:, k, P:2 * P]
                            nc.tensor.matmul(step[:, 0:P], ring[:, k, 0:P], onehot[:, k, :], start=True, stop=True)
                            last = nc.tensor.matmul(step[:, P:2 * P], second, onehot[:, k, :], start=True, stop=True)
                        last.then_inc(s_sum, 1)
                with if_irregular(pe):
                    with pe.Fori(LATE * layer, LATE * (layer + 1)) as t:
                        pe.wait_ge(s_late_rows, t * 16 + 16)
                        pe.wait_ge(s_late_hot, t + 1)
                        nc.tensor.matmul(ps[:, 0, 0:P], ring[:, 0, 0:P], onehot[:, 0, :], start=True, stop=True)
                        second = ones[:, :] if layer == 0 else ring[:, 0, P:2 * P]
                        nc.tensor.matmul(ps[:, 0, P:2 * P], second, onehot[:, 0, :], start=True,
                                         stop=True).then_inc(s_late_sum, 1)

            sum_edges(0)

            pe.wait_ge(s_weights, 16 * 13)

            def z_mean_part(n, u):
                pe.wait_ge(s_mean, n + 1)
                for m in range(2):
                    last = nc.tensor.matmul(ps[:, u, m * CH:(m + 1) * CH], w0[:, 0, m * P:(m + 1) * P],
                                            big[:, 1, ds(n * CH, CH)], start=False, stop=True, skip_group_check=True)
                last.then_inc(s_zmm, 1)

            def z_chunk(n, u, t):
                wait(pe, s_z, (n - (WIDE - 1)) * 2)
                for m in range(2):
                    nc.tensor.matmul(ps[:, u, m * CH:(m + 1) * CH], w0[:, 1, m * P:(m + 1) * P],
                                     big[:, 0, ds(n * CH, CH)], start=(m == 0), stop=False, skip_group_check=True)
                if not isinstance(n, int) or n >= Z_LAG:
                    z_mean_part(n - Z_LAG, (u - Z_LAG) % WIDE)
            Z_LAG = 6
            pe.wait_ge(s_summed, 1)
            each_chunk(pe, z_chunk, WIDE)
            for n in range(CHUNKS - Z_LAG, CHUNKS):
                z_mean_part(n, n % WIDE)
            pe.wait_ge(s_z, 2 * CHUNKS)

            def rows_and_self(n, u, t):
                pe.wait_ge(s_h, (n + 1) * 2)
                wait(pe, s_rowev, n - (DEPTH - 1))
                for j in range(2):
                    for k in range(2):
                        last = nc.tensor.matmul(ps[:, u, j * HID:(j + 1) * HID], h_stage[:, u, k, j * P:(j + 1) * P],
                                                w1[:, 0, k, :], start=(k == 0), stop=(k == 1))
                last.then_inc(s_rowmm, 1)
                wait(pe, s_selfev, (n - (DEPTH - 1)) * 2)
                for m in range(2):
                    for k in range(2):
                        last = nc.tensor.matmul(ps[:, 4 + u, m * CH:(m + 1) * CH], w1[:, 1, k, m * P:(m + 1) * P],
                                                h_stage[:, u, k, :], start=(k == 0), stop=(k == 1))
                last.then_inc(s_selfmm, 1)
            each_chunk(pe, rows_and_self)
            pe.wait_ge(s_rowev, CHUNKS)
            pe.wait_ge(s_selfev, 2 * CHUNKS)
            sum_edges(1)

            def rows_2(n, u, t):
                pe.wait_ge(s_h2, (n + 1) * 2)
                wait(pe, s_self2, n - (DEPTH - 1))
                for j in range(2):
                    for k in range(2):
                        nc.tensor.matmul(ps[:, u, j * OUT_C:(j + 1) * OUT_C], h_stage[:, u, k, j * P:(j + 1) * P],
                                         w2[:, k, 0:OUT_C], start=(k == 0), stop=(k == 1))
                for k in range(2):
                    last = nc.tensor.matmul(ps[:, 4 + u, 0:CH], w2[:, k, OUT_C:2 * OUT_C], h_stage[:, u, k, :],
                                            start=(k == 0), stop=(k == 1))
                last.then_inc(s_pmm, 1)
            each_chunk(pe, rows_2)
            pe.wait_ge(s_self2, CHUNKS)
            sum_edges(2)

            def transpose_result(n, u, t):
                pe.wait_ge(s_fin, n + 1)
                wait(pe, s_res, n - (DEPTH - 1))
                for j in range(2):
                    last = nc.tensor.transpose(ps[:, u, j * P:(j + 1) * P], h_stage[:, u, 0, j * P:(j + 1) * P],
                                               ident[:, :])
                last.then_inc(s_finT, 1)
            each_chunk(pe, transpose_result)

        @block.vector
        def _(dve):
            V = nc.vector
            done = {s_dve: 0, s_sort: 0}

            def link(ins, s=s_dve):
                done[s] += 1
                ins.then_inc(s, 1)
                dve.wait_ge(s, done[s])

            dve.sem_inc(s_acc, PER_IT)
            dve.wait_ge(s_const, 6)
            link(V.tensor_scalar(ident[:, :], iota_row[:, :], part_col[:, 0:1], None, ALU.is_equal))

            dve.wait_ge(s_dst, 48)
            dst_tiles = dst_nat.rearrange("p (c e) -> p c e", e=P)
            link(V.tensor_scalar(first_node[:, :], dst_tiles[:, :, 0], float(PADDED - P), None, ALU.min))

            def places_in_windows(last_one):
                for c in range(KCH):
                    ins = V.tensor_scalar(rel_f[:, c * P:(c + 1) * P], dst_nat[:, c * P:(c + 1) * P],
                                          first_node[:, c:c + 1], None, ALU.subtract)
                last_one(ins)
            places_in_windows(link)

            link(V.tensor_scalar(inside, rel_f, 0.0, None, ALU.is_ge))
            link(V.scalar_tensor_tensor(out=inside, in0=rel_f, scalar=float(P), in1=inside, op0=ALU.is_lt, op1=ALU.mult))
            V.reduce_sum(inside_sum, inside, mybir.AxisListType.X).then_inc(s_insides, 1)
            dve.wait_ge(s_total, 1)
            V.tensor_scalar(outside[:, :], ps[:, 0, 0:1], -1.0, float(EDGES), ALU.mult, ALU.add).then_inc(s_outside, 1)
            with if_irregular(dve):
                dve.wait_ge(s_by_edge, 32)
                dve.wait_ge(s_src, 48)
                V.tensor_scalar(is_before, iota_row[:, :], part_col[:, 0:1], None, ALU.is_gt)
                V.tensor_copy(bucket_no, iota_row[:, 0:BUCKETS])
                V.memset(counts, 0.0)
                link(V.tensor_scalar(bucket_i, dst_by_edge, P.bit_length() - 1, None, ALU.arith_shift_right), s_sort)
                link(V.tensor_scalar(bucket, bucket_i, float(BUCKETS - 1), None, ALU.min), s_sort)
                with dve.Fori(0, TAB_ROWS) as t:
                    V.tensor_scalar(in_bucket, bucket_no, bucket[:, ds(t, 1)], None, ALU.is_equal).then_inc(s_onehot, 1)
                    dve.wait_ge(s_tally, t + 1)
                    V.tensor_tensor(counts, counts, ps[:, 0, 0:BUCKETS], ALU.add).then_inc(s_tallied, 1)
                    dve.wait_ge(s_tallied, t + 1)
                link(V.tensor_tensor_scan(base, ones[:, 0:BUCKETS], counts, 0.0, ALU.mult, ALU.add), s_sort)
                link(V.tensor_tensor(base, base, counts, ALU.subtract), s_sort)
                with dve.Fori(TAB_ROWS, 2 * TAB_ROWS) as t:
                    V.tensor_scalar(in_bucket, bucket_no, bucket[:, ds(t - TAB_ROWS, 1)], None,
                                    ALU.is_equal).then_inc(s_onehot, 1)
                    dve.wait_ge(s_tally, t + 1)
                    V.tensor_tensor(before, base, ps[:, 1, 0:BUCKETS], ALU.add).then_inc(s_tallied, 1)
                    dve.wait_ge(s_tallied, t * 4 - (4 * TAB_ROWS - TAB_ROWS - 1))
                    V.tensor_tensor(base, base, ps[:, 0, 0:BUCKETS], ALU.add)
                    V.tensor_tensor(earlier, before, in_bucket, ALU.mult).then_inc(s_tallied, 1)
                    dve.wait_ge(s_tallied, t * 4 - (4 * TAB_ROWS - TAB_ROWS - 2))
                    V.reduce_sum(place, earlier, mybir.AxisListType.X).then_inc(s_tallied, 1)
                    V.tensor_copy(moved[:, 0:1], src_by_edge[:, ds(t - TAB_ROWS, 1)])
                    V.tensor_copy(moved[:, 1:2], dst_by_edge[:, ds(t - TAB_ROWS, 1)])
                    dve.wait_ge(s_tallied, t * 4 - (4 * TAB_ROWS - TAB_ROWS - 3))
                    V.tensor_copy(place_i, place).then_inc(s_tallied, 1)
                    dve.wait_ge(s_tallied, t * 4 - (4 * TAB_ROWS - TAB_ROWS - 4))
                    dve.sem_inc(s_place, 1)
                    dve.wait_ge(s_moved, t * 32 - (TAB_ROWS * 32 - 32))

                dve.wait_ge(s_firsts, 16)
                link(V.tensor_copy(firsts_f[:, :], firsts[:, :]), s_sort)
                for c in range(KCH):
                    V.tensor_scalar(starts_below[:, c, :], block_end[:, :], firsts_f[:, c:c + 1], None,
                                    ALU.is_gt).then_inc(s_cmp, 1)
                dve.wait_ge(s_counts, 1)
                link(V.tensor_scalar(ends[:, :], ps[:, 0, 0:BLOCKS - 1], 1.0, None, ALU.max), s_sort)
                link(V.tensor_tensor(ends[:, :], ends[:, :], block_no[:, :], ALU.add), s_sort)
                for c in range(KCH):
                    left = V.tensor_scalar(below[:, c, :], ends[:, :], step_no[:, c:c + 1], 0.0, ALU.is_le, ALU.add,
                                           accum_out=block_of[:, c:c + 1])
                    if c == KCH - 1:
                        link(left, s_sort)
                link(V.tensor_scalar(first_node[:, :], block_of[:, :], float(P), None, ALU.mult), s_sort)
                link(V.tensor_tensor(tile_no[:, :], step_no[:, :], block_of[:, :], ALU.subtract), s_sort)
                dve.sem_inc(s_ids, 1)
                dve.wait_ge(s_nat, 16 * 2 * KCH)
                places_in_windows(lambda ins: link(ins, s_sort))

            link(V.tensor_copy(first_node_i[:, :], first_node[:, :]))
            dve.sem_inc(s_windows, 1)
            dve.wait_ge(s_src, 48)
            V.tensor_copy(src_f, src_nat).then_inc(s_natf, 1)
            flat_ps = ps[:, :, :].rearrange("p a b -> p (a b)")
            for k, to in enumerate((idx_all, rel_all)):
                dve.wait_ge(s_edgeT, k + 1)
                V.tensor_copy(to[:, :], flat_ps[:, k * 2048:k * 2048 + STEPS]).then_inc(s_edges, 1)

            def layer_norm(g):
                dve.wait_ge(s_x[g], 32 if g == GROUPS - 1 else 16)
                first, end = group(g)

                def block_stats(into, blocks, count):
                    for j in range(count):
                        V.bn_stats(into[:, j, :], blocks[:, j, :]).then_inc(s_lnst, 1)
                with dve.Fori(first // DEPTH, end // DEPTH) as q:
                    block_stats(stats[:, ds(q * (2 * DEPTH), 2 * DEPTH), :], x_nat[:, ds(q * (2 * DEPTH), 2 * DEPTH), :],
                                2 * DEPTH)
                left = 2 * (end % DEPTH)
                block_stats(stats[:, 2 * end - left:2 * end, :], x_nat[:, 2 * end - left:2 * end, :], left)
                first, end = 2 * first, 2 * end
                dve.wait_ge(s_lnst, end)
                mean_g, half_diff, rstd_g, stats_g = mv[:, first:end, 0], mv[:, first:end, 1], rstd[:, first:end], stats[:, first:end]
                link(V.tensor_tensor(mean_g, stats_g[:, :, 1], stats_g[:, :, 4], ALU.add))
                link(V.tensor_scalar(mean_g, mean_g, 0.5, None, ALU.mult))
                link(V.tensor_tensor(half_diff, mean_g, stats_g[:, :, 4], ALU.subtract))
                link(V.tensor_tensor(half_diff, half_diff, half_diff, ALU.mult))
                link(V.tensor_tensor(rstd_g, stats_g[:, :, 2], stats_g[:, :, 5], ALU.add))
                link(V.scalar_tensor_tensor(out=rstd_g, in0=rstd_g, scalar=1.0 / IN_C, in1=half_diff,
                                            op0=ALU.mult, op1=ALU.add))
                V.tensor_scalar(rstd_g, rstd_g, EPS, None, ALU.add).then_inc(s_var, 1)
                dve.wait_ge(s_sd, g + 1)
                link(V.reciprocal(rstd_g, rstd_g))
                V.scalar_tensor_tensor(out=nbias[:, first:end], in0=mean_g, scalar=-1.0, in1=rstd_g,
                                       op0=ALU.mult, op1=ALU.mult).then_inc(s_lncoef, 1)

            def keep_h0T(n, u, t):
                dve.wait_ge(s_h0T, n + 1)
                V.tensor_copy(big[:, 0, ds(n * CH, CH)], ps[:, u, 0:CH]).then_inc(s_h0ev, 1)

            layer_norm(0)
            each_chunk(dve, keep_h0T, WIDE, before=lambda g: layer_norm(g + 1) if g + 1 < GROUPS else None)

            for g in range(GROUPS):
                first, end = group(g)
                dve.wait_ge(s_h0, 2 * end)
                V.memset(big[:, 1, first * CH:end * CH], 0.0).then_inc(s_zero, 1)
            dve.wait_ge(s_node_row, 16)
            dve.wait_ge(s_zero, GROUPS + 1)

            def hot(layer, i, h, j, node):
                if j == 0:
                    dve.wait_ge(s_sum, i * 2 + (2 * ITERS * layer + h + 1))
                k = h * HALF + j
                rel = rel_all[:, ds(i * PER_IT + k, 1)]
                if layer == 0:
                    ins = V.tensor_scalar(onehot[:, k, :], iota_row[:, :], rel, None, ALU.is_equal)
                else:
                    ins = V.scalar_tensor_tensor(out=onehot[:, k, :], in0=iota_row[:, :], scalar=rel,
                                                 in1=big[:, 2, ds(node, P)], op0=ALU.is_equal, op1=ALU.mult)
                if j == HALF - 1:
                    ins.then_inc(s_hot, 1)

            def accumulate(layer, i, h, j, node):
                if j == 0:
                    dve.wait_ge(s_sum, i * 2 + (2 * ITERS * layer + h + 3))
                k = h * HALF + j
                dve.wait_ge(s_acc, i * PER_IT + (PER_IT * ITERS * layer + PER_IT + k))
                step = ps[:, k // 2, (k % 2) * 256:(k % 2) * 256 + 256]
                if layer == 2:
                    sums = big[:, 0, ds(node, P)]
                    V.tensor_tensor(sums, sums, step[:, 0:P], ALU.add).then_inc(s_acc, 1)
                else:
                    first = 1 if layer == 0 else 0
                    sums = big[:, first:first + 2, ds(node, P)]
                    V.tensor_tensor(sums, sums, step.rearrange("p (m c) -> p m c", m=2), ALU.add).then_inc(s_acc, 1)

            def nodes_of(first, count):
                _, values = nc.values_load_multi_w_load_instructions(
                    node_row[0:1, ds(first, count)], engines=[mybir.EngineType.DVE],
                    min_val=0, max_val=PADDED - P,
                    skip_runtime_bounds_check_because="a window starts at a node or a block, and at most at PADDED - P")
                return values

            def sum_edges(layer):
                nodes = nodes_of(0, PER_IT)
                for h in range(2):
                    for j in range(HALF):
                        hot(layer, 0, h, j, nodes[h * HALF + j])
                with dve.Fori(0, ITERS - 1) as i:
                    nodes = nodes_of(i * PER_IT, 2 * PER_IT)
                    for h in range(2):
                        for j in range(HALF):
                            accumulate(layer, i, h, j, nodes[h * HALF + j])
                            hot(layer, i + 1, h, j, nodes[PER_IT + h * HALF + j])
                nodes = nodes_of(MAIN - PER_IT, PER_IT)
                for h in range(2):
                    for j in range(HALF):
                        accumulate(layer, ITERS - 1, h, j, nodes[h * HALF + j])
                dve.wait_ge(s_acc, PER_IT + PER_IT * ITERS * (layer + 1))
                with if_irregular(dve):
                    with dve.Fori(0, LATE) as t:
                        node = nodes_of(t + MAIN, 1)[0]
                        count = t + (LATE * layer + 1)
                        V.tensor_copy(idx_now[:, 0, 0:1], idx_all[:, ds(t + MAIN, 1)]).then_inc(s_late_idx, 1)
                        rel = rel_all[:, ds(t + MAIN, 1)]
                        if layer == 0:
                            V.tensor_scalar(onehot[:, 0, :], iota_row[:, :], rel, None, ALU.is_equal).then_inc(s_late_hot, 1)
                        else:
                            V.scalar_tensor_tensor(out=onehot[:, 0, :], in0=iota_row[:, :], scalar=rel,
                                                   in1=big[:, 2, ds(node, P)], op0=ALU.is_equal,
                                                   op1=ALU.mult).then_inc(s_late_hot, 1)
                        dve.wait_ge(s_late_sum, count)
                        sections, step = (slice(0, 1), ps[:, 0, 0:P]) if layer == 2 else \
                            (slice(1, 3) if layer == 0 else slice(0, 2), ps[:, 0, 0:2 * P])
                        sums = big[:, sections, ds(node, P)]
                        V.tensor_tensor(sums, sums, step.rearrange("p (m c) -> p m c", c=P), ALU.add).then_inc(s_late_acc, 1)
                        dve.wait_ge(s_late_acc, count)
                dve.sem_inc(s_summed, 1)

            sum_edges(0)

            dve.wait_ge(s_degree, 16)
            link(V.tensor_scalar(degrees[:, :], degrees[:, :], 1.0, None, ALU.max))
            V.reciprocal(degrees[:, :], degrees[:, :]).then_inc(s_inv, 1)

            def chunk_stats(n):
                c = LAST_COLS if last_chunk(n) else CH
                into, values = stats[:, ds(n * 2, 2), :], big[:, 0:2, ds(n * CH, c)]
                for m in range(2):
                    V.bn_stats(into[:, m, :], values[:, m, :]).then_inc(s_bnst, 1)

            LAG = 3

            def mean_and_stats(n, u, t):
                both = big[:, 1:3, ds(n * CH, CH)]
                V.tensor_tensor(both[:, 0, :], both[:, 0, :], both[:, 1, :], ALU.mult).then_inc(s_mean, 1)
                if not isinstance(n, int) or n >= LAG:
                    dve.wait_ge(s_z, (n - (LAG - 1)) * 2)
                    chunk_stats(n - LAG)
            each_chunk(dve, mean_and_stats, WIDE, before=lambda g: dve.wait_ge(s_inv_all[g], 16))
            for n in range(CHUNKS - LAG, CHUNKS):
                dve.wait_ge(s_z, (n + 1) * 2)
                chunk_stats(n)

            def batch_norm(layer):
                dve.wait_ge(s_bnst, 2 * CHUNKS * (layer + 1))
                for m in range(2):
                    link(V.bn_aggr(bn_mv[:, m, :],
                                   stats[:, :, :].rearrange("p (n m) s -> p m n s", m=2)[:, m]))
                V.tensor_scalar(bn_tmp[:, :], bn_mv[:, :, 1], EPS, None, ALU.add).then_inc(s_bnvar, 1)
                dve.wait_ge(s_bnsd, layer + 1)
                link(V.reciprocal(bn_tmp[:, :], bn_tmp[:, :]))
                link(V.tensor_tensor(bn_scale[:, :], bn_tmp[:, :], cols[:, 3 * layer + 1, :], ALU.mult))
                link(V.tensor_tensor(bn_tmp[:, :], bn_mv[:, :, 0], bn_scale[:, :], ALU.mult))
                V.tensor_tensor(bn_shift[:, :], cols[:, 3 * layer + 2, :], bn_tmp[:, :], ALU.subtract).then_inc(s_bn, 1)
            dve.wait_ge(s_weights, 16 * 13)
            batch_norm(0)

            def keep_rows_1(n, u, t):
                dve.wait_ge(s_rowmm, n + 1)
                wait(dve, s_row_out[u], t * 16)
                V.tensor_copy(row_stage[:, u].rearrange("p j c -> p (j c)"), ps[:, u, :]).then_inc(s_rowev, 1)
                dve.wait_ge(s_selfmm, n + 1)
                own = big[:, 0:2, ds(n * CH, CH)]
                for m in range(2):
                    V.tensor_scalar(own[:, m, :], ps[:, 4 + u, m * CH:(m + 1) * CH], cols[:, 3, m:m + 1],
                                    None, ALU.add).then_inc(s_selfev, 1)
            each_chunk(dve, keep_rows_1)
            dve.wait_ge(s_selfev, 2 * CHUNKS)
            sum_edges(1)

            each_chunk(dve, lambda n, u, t: chunk_stats(n))
            batch_norm(1)

            def keep_rows_2(n, u, t):
                dve.wait_ge(s_pmm, n + 1)
                wait(dve, s_p_out[u], t * 16)
                V.tensor_copy(row_stage[:, u, 0, :], ps[:, u, 0:CH]).then_inc(s_pev, 1)
                V.tensor_scalar(big[:, 0, ds(n * CH, CH)], ps[:, 4 + u, 0:CH], bl2_col[:, 0:1], None,
                                ALU.add).then_inc(s_self2, 1)
            each_chunk(dve, keep_rows_2)
            dve.wait_ge(s_self2, CHUNKS)
            sum_edges(2)

            dve.wait_ge(s_x_again, 16 * (OUT_PARTS + 1))

            def add_result(n, u, t):
                dve.wait_ge(s_finT, n + 1)
                here = big[:, 1, ds(n * CH, CH)]
                V.tensor_tensor(here, here, ps[:, u, 0:CH], ALU.add).then_inc(s_res, 1)
            each_chunk(dve, add_result)


_INS = ["x", "src", "dst", "L0_gnn_Wl0", "L0_gnn_bl0", "L0_gnn_Wr0", "L0_gnn_g0", "L0_gnn_b0", "L0_gnn_Wl1",
        "L0_gnn_bl1", "L0_gnn_Wr1", "L0_gnn_g1", "L0_gnn_b1", "L0_gnn_Wl2", "L0_gnn_bl2", "L0_gnn_Wr2"]


def kernel(**inputs):
    import numpy as _np
    import concourse.bacc as _bacc
    from concourse import mybir as _mybir
    from concourse.bass_utils import run_bass_kernel_spmd as _run

    nc = _bacc.Bacc("TRN2", target_bir_lowering=False, num_devices=1)
    arrays, args = {}, []
    for name in _INS:
        a = _np.ascontiguousarray(inputs[name])
        arrays[f"in_{name}"] = a
        args.append(nc.dram_tensor(f"in_{name}", a.shape, _mybir.dt.from_np(a.dtype), kind="ExternalInput").ap())
    args.append(nc.dram_tensor("out_0", (NODES, OUT_C), _mybir.dt.float32, kind="ExternalOutput").ap())
    gnn_kernel(nc, *args)
    r = _run(nc, [arrays], core_ids=[0])
    return r.results[0]["out_0"]
```

```python
import concourse.bass as bass
from concourse import mybir
from contextlib import ExitStack

P = 128
NODES = 12500
EDGES = 200000
IN_C, HID, OUT_C = 128, 256, 128
EPS = 1e-5

BLOCKS = -(-NODES // P)
PADDED = BLOCKS * P
LAST_ROWS = NODES - (BLOCKS - 1) * P
TILES = -(-EDGES // P)
WALK = TILES + BLOCKS - 1
KCH = -(-WALK // P)
STEPS = KCH * P
HALF = 8
PER_IT = 2 * HALF
PART = HALF // 2
IN_TURN = (PER_IT, PER_IT - 1, PER_IT)
ITERS = [-(-TILES // n) for n in IN_TURN]
BASE = [sum(ITERS[:layer]) for layer in range(4)]
MAIN = [n * t for n, t in zip(IN_TURN, ITERS)]
LATE = [STEPS - m for m in MAIN]
LATE_BASE = [sum(LATE[:layer]) for layer in range(3)]
assert min(LATE) >= 0 and min(ITERS) >= BLOCKS
FULL_C = TILES // P
FULL_TILES = EDGES // P - FULL_C * P
LEFT = EDGES % P
TAB_ROWS = STEPS
PAD_EDGES = TAB_ROWS * P - EDGES
BUCKETS = BLOCKS + 1
NO_NODE = 1 << 20
CH = 2 * P
CHUNKS = PADDED // CH
DEPTH = 8
ROW_DEPTH = 4
GROUPS = 3
OUT_PARTS = 7
LAST_COLS = NODES - (CHUNKS - 1) * CH


def gnn_kernel(nc, x, src, dst, Wl0, bl0, Wr0, g0, b0, Wl1, bl1, Wr1, g1, b1, Wl2, bl2, Wr2, out):
    f32 = mybir.dt.float32
    i32 = mybir.dt.int32
    u32 = mybir.dt.uint32
    ALU = mybir.AluOpType
    ACT = mybir.ActivationFunctionType
    ds = bass.ds

    ctx = ExitStack()
    with ctx:
        def sb(name, shape, dt=f32):
            return ctx.enter_context(nc.sbuf_tensor(name, shape, dt))

        def sem(name):
            return ctx.enter_context(nc.semaphore(name))

        def dram(name, shape, dt=f32):
            return nc.dram_tensor(name, shape, dt, kind="Internal").ap()

        src_tab = dram("src_tab", [TAB_ROWS, P], i32)
        dst_tab = dram("dst_tab", [TAB_ROWS, P], i32)
        node_dram = dram("node_dram", [STEPS], i32)
        input_dram = [None, dram("input1", [CHUNKS, P, 2 * CH]), dram("input2", [CHUNKS, P, 2 * CH])]
        degree_dram = dram("degree_dram", [PADDED])
        inverse_dram = dram("inverse_dram", [PADDED])
        table = [dram("table0", [PADDED, IN_C]), dram("table1", [PADDED, HID]), dram("table2", [PADDED, OUT_C])]

        big = sb("big", [P, 3, PADDED])
        ring = sb("ring", [P, PER_IT, HID])
        onehot = sb("onehot", [P, PER_IT, P])
        idx_all = sb("idx_all", [P, STEPS], i32)
        rel_all = sb("rel_all", [P, STEPS])
        node_row = sb("node_row", [1, STEPS], i32)
        idx_now = sb("idx_now", [P, 2, HALF], i32)
        w0 = sb("w0", [P, 2, HID])
        w1 = sb("w1", [P, 2, 2, HID])
        w2 = sb("w2", [P, 2, 2 * OUT_C])
        cols = sb("cols", [P, 6, 2])
        bl2_col = sb("bl2_col", [P, 1])
        iota_row = sb("iota_row", [P, P])
        part_col = sb("part_col", [P, 1])
        ident = sb("ident", [P, P])
        ones = sb("ones", [P, P])
        block_end = sb("block_end", [P, BLOCKS - 1])
        block_no = sb("block_no", [P, BLOCKS - 1])
        step_no = sb("step_no", [P, KCH])
        pads = sb("pads", [P, 2, P], i32)
        degrees = sb("degrees", [P, BLOCKS])
        firsts = sb("firsts", [P, KCH], i32)
        firsts_f = sb("firsts_f", [P, KCH])
        ends = sb("ends", [P, BLOCKS - 1])
        block_of = sb("block_of", [P, KCH])
        first_node = sb("first_node", [P, KCH])
        first_node_i = sb("first_node_i", [P, KCH], i32)
        tile_no = sb("tile_no", [P, KCH], i32)
        stats = sb("stats", [P, 2 * CHUNKS, 6])
        rstd = sb("rstd", [P, BLOCKS])
        bn_mv = sb("bn_mv", [P, 2, 2])
        bn_scale = sb("bn_scale", [P, 2])
        bn_shift = sb("bn_shift", [P, 2])
        bn_tmp = sb("bn_tmp", [P, 2])
        outside = sb("outside", [P, 1], i32)

        h0_stage = ring[:, PER_IT - DEPTH:PER_IT, :]
        h_stage = ring[:, :, :].rearrange("p (u j) c -> p u j c", u=DEPTH)
        row_stage = [None, onehot[:, :, :].rearrange("p (b a) c -> p b (a c)", a=HID // P), onehot]
        own_slot = [None, ring[:, PER_IT - 1, :].rearrange("p (k c) -> p k c", k=2), ring[:, PER_IT - 2:PER_IT, P:2 * P]]
        src_nat = big[:, 2, 0:STEPS].bitcast(i32)
        dst_nat = big[:, 2, STEPS:2 * STEPS].bitcast(i32)
        src_f = big[:, 2, 2 * STEPS:3 * STEPS]
        rel_f = big[:, 2, 3 * STEPS:4 * STEPS]
        starts_below = big[:, 2, 4 * STEPS:4 * STEPS + KCH * (BLOCKS - 1)].rearrange("p (c b) -> p c b", c=KCH)
        below = big[:, 2, 6 * STEPS:6 * STEPS + KCH * (BLOCKS - 1)].rearrange("p (c b) -> p c b", c=KCH)
        inside = big[:, 2, 4 * STEPS:5 * STEPS]
        src_by_edge, dst_by_edge = (big[:, 0, k * STEPS:(k + 1) * STEPS].bitcast(i32) for k in range(2, 4))
        bucket_i = big[:, 0, 4 * STEPS:5 * STEPS].bitcast(i32)
        bucket = big[:, 0, 5 * STEPS:6 * STEPS]
        sort_area = big[:, 0, 6 * STEPS:6 * STEPS + 8 * P].rearrange("p (k n) -> p k n", n=P)
        in_bucket, counts, base, before, earlier, bucket_no = (sort_area[:, k, 0:BUCKETS] for k in range(6))
        is_before = sort_area[:, 6, :]
        inside_sum, place = sort_area[:, 7, 0:1], sort_area[:, 7, 1:2]
        place_i = sort_area[:, 7, 2:3].bitcast(i32)
        moved = sort_area[:, 7, 3:5].bitcast(i32)

        ln_area = ring[:, 0:2, :].rearrange("p a c -> p (a c)")
        mv = ln_area[:, 0:2 * BLOCKS].rearrange("p (b s) -> p b s", s=2)
        nbias = ln_area[:, 2 * BLOCKS:3 * BLOCKS]
        x_nat = big[:, 1, :].rearrange("p (b f) -> p b f", f=IN_C)

        ps = ctx.enter_context(nc.psum_tensor("ps", [P, 8, 512], f32))

        s_const = sem("s_const")
        s_pads = sem("s_pads")
        s_weights = sem("s_weights")
        s_dst = sem("s_dst")
        s_src = sem("s_src")
        s_x = [sem(f"s_x{g}") for g in range(GROUPS)]
        s_insides = sem("s_insides")
        s_total = sem("s_total")
        s_outside = sem("s_outside")
        s_tabs = sem("s_tabs")
        s_by_edge = sem("s_by_edge")
        s_onehot = sem("s_onehot")
        s_tally = sem("s_tally")
        s_tallied = sem("s_tallied")
        s_place = sem("s_place")
        s_begin = sem("s_begin")
        s_moved = sem("s_moved")
        s_order = sem("s_order")
        s_firsts = sem("s_firsts")
        s_cmp = sem("s_cmp")
        s_counts = sem("s_counts")
        s_ids = sem("s_ids")
        s_nat = sem("s_nat")
        s_windows = sem("s_windows")
        s_row_made = sem("s_row_made")
        s_node_row = sem("s_node_row")
        s_natf = sem("s_natf")
        s_edgeT = sem("s_edgeT")
        s_edges = sem("s_edges")
        s_dve = sem("s_dve")
        s_sort = sem("s_sort")
        s_lnst = sem("s_lnst")
        s_var = sem("s_var")
        s_sd = sem("s_sd")
        s_lncoef = sem("s_lncoef")
        s_h0 = sem("s_h0")
        s_h0T = sem("s_h0T")
        s_h0ev = sem("s_h0ev")
        s_h0_out = [sem(f"s_h0_out{u}") for u in range(DEPTH)]
        s_tables = sem("s_tables")
        s_zero = sem("s_zero")
        s_idx = sem("s_idx")
        s_half = sem("s_half")
        s_rows = [sem(f"s_rows{k}") for k in range(PER_IT // PART)]
        s_hot = sem("s_hot")
        s_sum = sem("s_sum")
        s_acc = sem("s_acc")
        s_late_idx = sem("s_late_idx")
        s_late_begin = sem("s_late_begin")
        s_late_rows = sem("s_late_rows")
        s_late_hot = sem("s_late_hot")
        s_late_sum = sem("s_late_sum")
        s_late_acc = sem("s_late_acc")
        s_summed = sem("s_summed")
        s_degree_out = sem("s_degree_out")
        s_degree = sem("s_degree")
        s_inv = sem("s_inv")
        s_inv_out = sem("s_inv_out")
        s_inv_all = [sem(f"s_inv_all{g}") for g in range(GROUPS)]
        s_mean = sem("s_mean")
        s_zmm = sem("s_zmm")
        s_z = sem("s_z")
        s_bnst = sem("s_bnst")
        s_bnvar = sem("s_bnvar")
        s_bnsd = sem("s_bnsd")
        s_bn = sem("s_bn")
        s_h = sem("s_h")
        s_rowmm = sem("s_rowmm")
        s_rowev = sem("s_rowev")
        s_bias = sem("s_bias")
        s_input_out = [None] + [[sem(f"s_input{layer}_out{w}") for w in range(DEPTH // 2)] for layer in (1, 2)]
        s_own = sem("s_own")
        s_own_acc = sem("s_own_acc")
        s_row_out = [sem(f"s_row_out{w}") for w in range(ROW_DEPTH // 2)]
        s_h2 = sem("s_h2")
        s_pmm = sem("s_pmm")
        s_pev = sem("s_pev")
        s_bias2 = sem("s_bias2")
        s_p_out = [sem(f"s_p_out{w}") for w in range(ROW_DEPTH // 2)]
        s_x_again = sem("s_x_again")
        s_fin = sem("s_fin")
        s_finT = sem("s_finT")
        s_res = sem("s_res")
        s_out = sem("s_out")

        def uses(total, buffer, buffers):
            return -(-(total - buffer) // buffers)

        def each_chunk(eng, body, before=None):
            turns = CHUNKS // DEPTH
            for g in range(GROUPS if before else 1):
                first, last = (g * turns // GROUPS, (g + 1) * turns // GROUPS) if before else (0, turns)
                if before:
                    before(g)
                if g == 0:
                    for u in range(DEPTH):
                        body(u, u, 0)
                with eng.Fori(max(first, 1), last) as t:
                    for u in range(DEPTH):
                        body(t * DEPTH + u, u, t)
            body(CHUNKS - 1, 0, turns)

        def each_pair(eng, body):
            def chunk(n, u, t):
                if u % 2 == 0:
                    body(n, u, t, 1 if last_chunk(n) else 2)
            each_chunk(eng, chunk)

        def pairs_to(u, t):
            return t * (DEPTH // 2) + (u // 2 + 1)

        def group(g):
            turns = CHUNKS // DEPTH
            return g * turns // GROUPS * DEPTH, CHUNKS if g == GROUPS - 1 else (g + 1) * turns // GROUPS * DEPTH

        def in_half(layer, h):
            return min(HALF, IN_TURN[layer] - h * HALF)

        def half_free(layer, h, i):
            return i * 2 + (2 * BASE[layer] + h + 1)

        def wait(eng, s, value):
            if not isinstance(value, int) or value > 0:
                eng.wait_ge(s, value)

        def last_chunk(n):
            return isinstance(n, int) and n == CHUNKS - 1

        def if_irregular(eng):
            eng.wait_ge(s_outside, 1)
            return eng.If(nc.values_load(outside[0:1, 0:1], engines=[eng.engine], min_val=0, max_val=STEPS * P) > 0)

        block = ctx.enter_context(nc.Block())

        @block.sync
        def _(sp):
            sp.wait_ge(s_pads, 5)
            cols_end = FULL_C * P * P
            for edges, nat, loaded in ((dst, dst_nat, s_dst), (src, src_nat, s_src)):
                sp.dma_start(nat[:, 0:FULL_C * P].rearrange("p (c e) -> p c e", e=P),
                             edges[0:cols_end].rearrange("(c p e) -> p c e", p=P, e=P)).then_inc(loaded, 16)
                sp.dma_start(nat[0:FULL_TILES, FULL_C * P:(FULL_C + 1) * P],
                             edges[cols_end:cols_end + FULL_TILES * P].rearrange("(p e) -> p e", e=P)).then_inc(loaded, 16)
                sp.dma_start(nat[FULL_TILES:FULL_TILES + 1, FULL_C * P:FULL_C * P + LEFT],
                             edges[EDGES - LEFT:EDGES].rearrange("(a n) -> a n", a=1)).then_inc(loaded, 16)
            for g in range(GROUPS):
                first, end = (2 * n for n in group(g))
                full = min(end, BLOCKS - 1)
                sp.dma_start(x_nat[:, first:full, :],
                             x[first * P:full * P, :].rearrange("(b p) f -> p b f", p=P)).then_inc(s_x[g], 16)
            sp.dma_start(x_nat[0:LAST_ROWS, BLOCKS - 1, :], x[(BLOCKS - 1) * P:NODES, :]).then_inc(s_x[GROUPS - 1], 16)

            with if_irregular(sp):
                flat = [tab.rearrange("t e -> (t e)") for tab in (src_tab, dst_tab)]
                full = PAD_EDGES // P
                left = PAD_EDGES - full * P
                for k, (tab, edges) in enumerate(zip(flat, (src, dst))):
                    sp.dma_start(tab[0:EDGES].rearrange("(a n) -> a n", a=16),
                                 edges.rearrange("(a n) -> a n", a=16)).then_inc(s_tabs, 16)
                    sp.dma_start(tab[EDGES:EDGES + full * P].rearrange("(a n) -> a n", n=P),
                                 pads[0:full, k, :]).then_inc(s_tabs, 16)
                    sp.dma_start(tab[EDGES + full * P:EDGES + full * P + left].rearrange("(a n) -> a n", a=1),
                                 pads[0:1, k, 0:left]).then_inc(s_tabs, 16)
                sp.wait_ge(s_tabs, 16 * 6)
                with nc.allow_non_contiguous_dma(reason="only for edges that come unsorted"):
                    for tab, to in ((src_tab, src_by_edge), (dst_tab, dst_by_edge)):
                        sp.dma_start(to, tab[0:TAB_ROWS, :].rearrange("t e -> e t")).then_inc(s_by_edge, 16)
                sp.wait_ge(s_order, 1)
                with nc.allow_non_contiguous_dma(reason="one word of each tile"):
                    sp.dma_start(firsts[:, :], dst_tab[0:TAB_ROWS, 0].rearrange("(c p) -> p c", p=P)).then_inc(s_firsts, 16)

            sp.wait_ge(s_windows, 1)
            with nc.allow_non_contiguous_dma(reason="one word a step"):
                sp.dma_start(node_dram.rearrange("(c p) -> p c", p=P), first_node_i[:, :]).then_inc(s_row_made, 16)
            sp.wait_ge(s_row_made, 16)
            sp.dma_start(node_row[0:1, :], node_dram.rearrange("(a n) -> a n", a=1)).then_inc(s_node_row, 16)

            tb0 = table[0].rearrange("(b p) f -> p b f", p=P)

            def store_h0(n, u, t):
                sp.wait_ge(s_h0, (n + 1) * 2)
                sp.dma_start(tb0[:, ds(n * 2, 2), :],
                             h0_stage[:, u, :].rearrange("p (j f) -> p j f", j=2)).then_inc(s_h0_out[u], 16)
            each_chunk(sp, store_h0)
            for u in range(DEPTH):
                sp.wait_ge(s_h0_out[u], 16 * uses(CHUNKS, u, DEPTH))
            sp.sem_inc(s_tables, 1)

            sp.wait_ge(s_summed, 1)
            sp.dma_start(degree_dram.rearrange("(a n) -> a n", a=1), big[0:1, 2, :]).then_inc(s_degree_out, 16)
            sp.wait_ge(s_degree_out, 16)
            sp.dma_start(degrees[:, :], degree_dram.rearrange("(p j) -> p j", j=BLOCKS)).then_inc(s_degree, 16)
            sp.wait_ge(s_inv, 1)
            sp.dma_start(inverse_dram.rearrange("(p j) -> p j", j=BLOCKS), degrees[:, :]).then_inc(s_inv_out, 16)
            sp.wait_ge(s_inv_out, 16)
            for g in range(GROUPS):
                first, end = (CH * n for n in group(g))
                sp.dma_start(big[:, 2, first:end],
                             inverse_dram[first:end].rearrange("(a n) -> a n", a=1).to_broadcast([P, end - first])
                             ).then_inc(s_inv_all[g], 16)

            body_rows = (BLOCKS - 1) * P

            def stores(layer, staged, rows_staged, rows_out):
                to = table[layer].rearrange("(b p) f -> p b f", p=P)

                def store(n, u, t, count):
                    sp.wait_ge(staged, pairs_to(u, t) * 2)
                    sp.dma_start(input_dram[layer][ds(n, count)].rearrange("a p c -> p a c"),
                                 h_stage[:, u:u + count].rearrange("p a j c -> p a (j c)")
                                 ).then_inc(s_input_out[layer][u // 2], 16)
                    sp.wait_ge(rows_staged, n + count)
                    v = u % ROW_DEPTH
                    sp.dma_start(to[:, ds(n * 2, 2 * count), :],
                                 row_stage[layer][:, 2 * v:2 * (v + count), :]).then_inc(rows_out[v // 2], 16)
                each_pair(sp, store)
                pairs = (CHUNKS + 1) // 2
                for w in range(DEPTH // 2):
                    sp.wait_ge(s_input_out[layer][w], 16 * uses(pairs, w, DEPTH // 2))
                for w in range(ROW_DEPTH // 2):
                    sp.wait_ge(rows_out[w], 16 * uses(pairs, w, ROW_DEPTH // 2))
                sp.sem_inc(s_tables, 1)

            def load_own(layer, n, j):
                sp.wait_ge(s_sum, half_free(layer, 1, n * 2 + j))
                chunk = input_dram[layer][ds(n, 1)].rearrange("a p (k c) -> p (a k) c", k=2)
                sp.dma_start(own_slot[layer], chunk[:, :, j * P:(j + 1) * P]).then_inc(s_own, 16)

            stores(1, s_h, s_rowev, s_row_out)
            with sp.Fori(0, CHUNKS) as n:
                for j in range(2):
                    load_own(1, n, j)

            stores(2, s_h2, s_pev, s_p_out)
            with sp.Fori(0, CHUNKS - 1) as n:
                for j in range(2):
                    load_own(2, n, j)
                sp.dma_start(x_nat[:, ds(n * 2, 2), :],
                             x[ds(n * CH, CH), :].rearrange("(b p) f -> p b f", p=P)).then_inc(s_x_again, 16)
            for j in range(2):
                load_own(2, CHUNKS - 1, j)
            sp.dma_start(x_nat[:, BLOCKS - 2, :], x[body_rows - P:body_rows, :]).then_inc(s_x_again, 16)
            sp.dma_start(x_nat[0:LAST_ROWS, BLOCKS - 1, :], x[body_rows:NODES, :]).then_inc(s_x_again, 16)

            for part in range(OUT_PARTS):
                first, end = (b * BLOCKS // OUT_PARTS for b in (part, part + 1))
                sp.wait_ge(s_res, -(-end // 4))
                full = min(end, BLOCKS - 1)
                sp.dma_start(out[first * P:full * P, :].rearrange("(b p) f -> p b f", p=P),
                             x_nat[:, first:full, :]).then_inc(s_out, 16)
            sp.dma_start(out[body_rows:NODES, :], x_nat[0:LAST_ROWS, BLOCKS - 1, :]).then_inc(s_out, 16)
            sp.wait_ge(s_out, 16 * (OUT_PARTS + 1))

        @block.gpsimd
        def _(pool):
            pool.memset(pads[:, 0, :], 0).then_inc(s_pads, 1)
            pool.memset(pads[:, 1, :], NO_NODE).then_inc(s_pads, 1)
            pool.memset(dst_nat[:, FULL_C * P:(FULL_C + 1) * P], NO_NODE).then_inc(s_pads, 1)
            pool.memset(src_nat[:, FULL_C * P:(FULL_C + 1) * P], 0).then_inc(s_pads, 1)
            pool.memset(x_nat[:, BLOCKS - 1, :], 0.0).then_inc(s_pads, 1)
            f = dict(allow_small_or_imprecise_dtypes=True)
            pool.iota(iota_row[:, :], [[1, P]], base=0, channel_multiplier=0, **f).then_inc(s_const, 1)
            pool.iota(part_col[:, :], [[0, 1]], base=0, channel_multiplier=1, **f).then_inc(s_const, 1)
            pool.iota(block_end[:, :], [[P, BLOCKS - 1]], base=P, channel_multiplier=0, **f).then_inc(s_const, 1)
            pool.iota(block_no[:, :], [[1, BLOCKS - 1]], base=0, channel_multiplier=0, **f).then_inc(s_const, 1)
            pool.iota(step_no[:, :], [[P, KCH]], base=0, channel_multiplier=1, **f).then_inc(s_const, 1)
            pool.memset(ones[:, :], 1.0).then_inc(s_const, 1)

            with if_irregular(pool):
                with pool.Fori(0, TAB_ROWS) as t:
                    pool.wait_ge(s_place, t + 1)
                    pool.sem_inc(s_begin, 1)
                    for k, tab in enumerate((src_tab, dst_tab)):
                        pool.indirect_dma_start(
                            out=tab[0:TAB_ROWS, :].rearrange("t (e a) -> (t e) a", a=1),
                            out_offset=bass.IndirectOffsetOnAxis(ap=place_i.bitcast(u32), axis=0),
                            in_=moved[:, k:k + 1], in_offset=None).then_inc(s_moved, 16)
                    pool.wait_ge(s_moved, t * 32 + 32)
                pool.sem_inc(s_order, 1)
                pool.wait_ge(s_ids, 1)
                for c in range(KCH):
                    for tab, nat in ((src_tab, src_nat), (dst_tab, dst_nat)):
                        pool.indirect_dma_start(
                            out=nat[:, c * P:(c + 1) * P], out_offset=None, in_=tab[:, :],
                            in_offset=bass.IndirectOffsetOnAxis(ap=tile_no[:, c:c + 1].bitcast(u32), axis=0),
                        ).then_inc(s_nat, 16)

            pool.wait_ge(s_edges, 2)
            pool.memset(big[:, 2, :], 0.0).then_inc(s_zero, 1)

            for layer in range(3):
                width = table[layer].shape[1]
                pool.wait_ge(s_tables, layer + 1)
                with pool.Fori(0, ITERS[layer]) as i:
                    for h in range(2):
                        pool.wait_ge(s_idx, i * 2 + (2 * BASE[layer] + h + 1))
                        pool.sem_inc(s_half, 1)
                        for j in range(in_half(layer, h)):
                            pool.indirect_dma_start(
                                out=ring[:, h * HALF + j, 0:width], out_offset=None, in_=table[layer][:, :],
                                in_offset=bass.IndirectOffsetOnAxis(ap=idx_now[:, h, j:j + 1].bitcast(u32), axis=0),
                            ).then_inc(s_rows[(h * HALF + j) // PART], 16)
                with if_irregular(pool):
                    with pool.Fori(LATE_BASE[layer], LATE_BASE[layer] + LATE[layer]) as t:
                        pool.wait_ge(s_late_idx, t + 1)
                        pool.sem_inc(s_late_begin, 1)
                        pool.indirect_dma_start(
                            out=ring[:, 0, 0:width], out_offset=None, in_=table[layer][:, :],
                            in_offset=bass.IndirectOffsetOnAxis(ap=idx_now[:, 0, 0:1].bitcast(u32), axis=0),
                        ).then_inc(s_late_rows, 16)

        @block.scalar
        def _(act):
            for k, w in enumerate((Wl0, Wr0)):
                act.dma_start(w0[:, k, :], w).then_inc(s_weights, 16)
            for k, w in enumerate((Wl1, Wr1)):
                act.dma_start(w1[:, k], w.rearrange("(k p) n -> p k n", p=P)).then_inc(s_weights, 16)
            for k, w in enumerate((Wl2, Wr2)):
                act.dma_start(w2[:, :, k * OUT_C:(k + 1) * OUT_C],
                              w.rearrange("(k p) n -> p k n", p=P)).then_inc(s_weights, 16)
            with nc.allow_non_contiguous_dma(reason="vectors over the features"):
                for k, v in enumerate((bl0, g0, b0, bl1, g1, b1)):
                    act.dma_start(cols[:, k, :], v.rearrange("(m p) -> p m", p=P)).then_inc(s_weights, 16)
                act.dma_start(bl2_col[:, :], bl2.rearrange("(p a) -> p a", a=1)).then_inc(s_weights, 16)

            def group_sd(g):
                first, end = (2 * n for n in group(g))
                act.wait_ge(s_var, g + 1)
                nc.scalar.activation(rstd[:, first:end], rstd[:, first:end], ACT.Sqrt).then_inc(s_sd, 1)
                act.wait_ge(s_lncoef, g + 1)

            def normalise(n, u, t):
                wait(act, s_h0T, n - (DEPTH - 1))
                wait(act, s_h0_out[u], t * 16)
                blocks, biases, scales = (a[:, ds(n * 2, 2)] for a in (x_nat, nbias, rstd))
                for j in range(2):
                    nc.scalar.activation(h0_stage[:, u, j * P:(j + 1) * P], blocks[:, j, :], ACT.Relu,
                                         bias=biases[:, j:j + 1], scale=scales[:, j:j + 1]).then_inc(s_h0, 1)
            each_chunk(act, normalise, before=group_sd)
            act.wait_ge(s_h0T, CHUNKS)

            def stage_indices(layer):
                with act.Fori(0, ITERS[layer]) as i:
                    for h in range(2):
                        act.wait_ge(s_sum, half_free(layer, h, i))
                        n = in_half(layer, h)
                        nc.scalar.activation(idx_now[:, h, 0:n], idx_all[:, ds(i * IN_TURN[layer] + h * HALF, n)],
                                             ACT.Copy).then_inc(s_idx, 1)

            act.wait_ge(s_weights, 16 * 13)
            stage_indices(0)

            def evacuate_z(n, u, t):
                act.wait_ge(s_zmm, n + 1)
                z = big[:, 0:2, ds(n * CH, CH)]
                for m in range(2):
                    nc.scalar.activation(z[:, m, :], ps[:, u, m * CH:(m + 1) * CH], ACT.Identity,
                                         bias=cols[:, 0, m:m + 1]).then_inc(s_z, 1)
            each_chunk(act, evacuate_z)

            def batch_norm_sd(layer):
                act.wait_ge(s_bnvar, layer + 1)
                nc.scalar.activation(bn_tmp[:, :], bn_tmp[:, :], ACT.Sqrt).then_inc(s_bnsd, 1)
                act.wait_ge(s_bn, layer + 1)

            def relu_pair(layer, n, u, t, count, staged, read):
                wait(act, s_input_out[layer][u // 2], t * 16)
                wait(act, read, n + count - DEPTH)
                z = big[:, 0:2, ds(n * CH, count * CH)]
                for m in range(2):
                    nc.scalar.activation(h_stage[:, u:u + count, m, :],
                                         z[:, m, :].rearrange("p (j c) -> p j c", c=CH), ACT.Relu,
                                         bias=bn_shift[:, m:m + 1], scale=bn_scale[:, m:m + 1]).then_inc(staged, 1)

            batch_norm_sd(0)
            each_pair(act, lambda n, u, t, count: relu_pair(1, n, u, t, count, s_h, s_rowmm))
            act.wait_ge(s_rowmm, CHUNKS)
            stage_indices(1)

            batch_norm_sd(1)
            each_pair(act, lambda n, u, t, count: relu_pair(2, n, u, t, count, s_h2, s_pmm))
            act.wait_ge(s_pmm, CHUNKS)
            stage_indices(2)

            act.wait_ge(s_summed, 3)

            def stage_result(n, u, t, count):
                wait(act, s_finT, n + count - DEPTH)
                nc.scalar.activation(h_stage[:, u:u + count, 0, :],
                                     big[:, 0, ds(n * CH, count * CH)].rearrange("p (j c) -> p j c", c=CH),
                                     ACT.Copy).then_inc(s_fin, 1)
            each_pair(act, stage_result)

        @block.tensor
        def _(pe):
            pe.sem_inc(s_sum, 2)

            pe.wait_ge(s_const, 6)
            pe.wait_ge(s_insides, 1)
            nc.tensor.matmul(ps[:, 0, 0:1], ones[:, :], inside_sum, start=True, stop=True).then_inc(s_total, 1)
            with if_irregular(pe):
                with pe.Fori(0, TAB_ROWS) as t:
                    pe.wait_ge(s_onehot, t + 1)
                    nc.tensor.matmul(ps[:, 0, 0:BUCKETS], ones[:, :], in_bucket, start=True, stop=True).then_inc(s_tally, 1)
                with pe.Fori(TAB_ROWS, 2 * TAB_ROWS) as t:
                    pe.wait_ge(s_onehot, t + 1)
                    nc.tensor.matmul(ps[:, 0, 0:BUCKETS], ones[:, :], in_bucket, start=True, stop=True)
                    nc.tensor.matmul(ps[:, 1, 0:BUCKETS], is_before, in_bucket, start=True, stop=True).then_inc(s_tally, 1)

                pe.wait_ge(s_cmp, KCH)
                for c in range(KCH):
                    last = nc.tensor.matmul(ps[:, 0, 0:BLOCKS - 1], ones[:, :], starts_below[:, c, :],
                                            start=(c == 0), stop=(c == KCH - 1))
                last.then_inc(s_counts, 1)

            pe.wait_ge(s_natf, 1)
            pe.wait_ge(s_outside, 1)
            for k, nat in enumerate((src_f, rel_f)):
                for c in range(KCH):
                    last = nc.tensor.transpose(ps[:, 4 * k + c // 4, (c % 4) * P:(c % 4 + 1) * P],
                                               nat[:, c * P:(c + 1) * P], ident[:, :])
                last.then_inc(s_edgeT, 1)

            def transpose_h0(n, u, t):
                pe.wait_ge(s_h0, (n + 1) * 2)
                wait(pe, s_h0ev, n - (DEPTH - 1))
                for j in range(2):
                    last = nc.tensor.transpose(ps[:, u, j * P:(j + 1) * P], h0_stage[:, u, j * P:(j + 1) * P],
                                               ident[:, :])
                last.then_inc(s_h0T, 1)
            pe.wait_ge(s_edges, 2)
            each_chunk(pe, transpose_h0)
            pe.wait_ge(s_h0ev, CHUNKS)

            def sum_edges(layer):
                def landed(part, i):
                    count = [min(PART, IN_TURN[k] - part * PART) for k in range(3)]
                    return i * (16 * count[layer]) + 16 * (count[layer] + sum(ITERS[k] * count[k] for k in range(layer)))

                def turn(i, own):
                    for h in range(2):
                        pe.wait_ge(s_hot, i * 2 + (2 * BASE[layer] + h + 1))
                        pe.wait_ge(s_acc, i * PER_IT + (PER_IT * BASE[layer] + HALF * (h + 1)))
                        if layer == 2 and h == 1:
                            pe.wait_ge(s_own_acc, i + 1)
                        for j in range(in_half(layer, h)):
                            k = h * HALF + j
                            if k % PART == 0:
                                pe.wait_ge(s_rows[k // PART], landed(k // PART, i))
                            step = ps[:, k // 2, (k % 2) * 256:(k % 2) * 256 + 256]
                            if layer == 2:
                                last = nc.tensor.matmul(step[:, 0:P], ring[:, k, 0:OUT_C], onehot[:, k, :],
                                                        start=True, stop=True)
                                continue
                            second = ones[:, :] if layer == 0 else ring[:, k, P:2 * P]
                            nc.tensor.matmul(step[:, 0:P], ring[:, k, 0:P], onehot[:, k, :], start=True, stop=True)
                            last = nc.tensor.matmul(step[:, P:2 * P], second, onehot[:, k, :], start=True, stop=True)
                        if h == 1 and own:
                            pe.wait_ge(s_own, i * 16 + 16 * (BLOCKS * (layer - 1) + 1))
                            to = ps[:, 7, 256:512]
                            if layer == 1:
                                for m in range(2):
                                    for k in range(2):
                                        last = nc.tensor.matmul(to[:, m * P:(m + 1) * P], w1[:, 1, k, m * P:(m + 1) * P],
                                                                own_slot[1][:, k, :], start=(k == 0), stop=(k == 1))
                            else:
                                for k in range(2):
                                    last = nc.tensor.matmul(to[:, P:2 * P], w2[:, k, OUT_C:2 * OUT_C],
                                                            own_slot[2][:, k, :], start=(k == 0), stop=(k == 1))
                        last.then_inc(s_sum, 1)

                with pe.Fori(0, BLOCKS if layer else ITERS[0]) as i:
                    turn(i, layer > 0)
                if layer and ITERS[layer] > BLOCKS:
                    with pe.Fori(BLOCKS, ITERS[layer]) as i:
                        turn(i, False)
                with if_irregular(pe):
                    with pe.Fori(LATE_BASE[layer], LATE_BASE[layer] + LATE[layer]) as t:
                        pe.wait_ge(s_late_rows, t * 16 + 16)
                        pe.wait_ge(s_late_hot, t + 1)
                        nc.tensor.matmul(ps[:, 0, 0:P], ring[:, 0, 0:P], onehot[:, 0, :], start=True, stop=True)
                        second = ones[:, :] if layer == 0 else ring[:, 0, P:2 * P]
                        nc.tensor.matmul(ps[:, 0, P:2 * P], second, onehot[:, 0, :], start=True,
                                         stop=True).then_inc(s_late_sum, 1)

            sum_edges(0)

            Z_LAG = 6
            pe.wait_ge(s_weights, 16 * 13)

            def z_mean_part(n, u):
                pe.wait_ge(s_mean, n + 1)
                for m in range(2):
                    last = nc.tensor.matmul(ps[:, u, m * CH:(m + 1) * CH], w0[:, 0, m * P:(m + 1) * P],
                                            big[:, 1, ds(n * CH, CH)], start=False, stop=True, skip_group_check=True)
                last.then_inc(s_zmm, 1)

            def z_chunk(n, u, t):
                wait(pe, s_z, (n - (DEPTH - 1)) * 2)
                for m in range(2):
                    nc.tensor.matmul(ps[:, u, m * CH:(m + 1) * CH], w0[:, 1, m * P:(m + 1) * P],
                                     big[:, 0, ds(n * CH, CH)], start=(m == 0), stop=False, skip_group_check=True)
                if not isinstance(n, int) or n >= Z_LAG:
                    z_mean_part(n - Z_LAG, (u - Z_LAG) % DEPTH)
            pe.wait_ge(s_summed, 1)
            each_chunk(pe, z_chunk)
            for n in range(CHUNKS - Z_LAG, CHUNKS):
                z_mean_part(n, n % DEPTH)
            pe.wait_ge(s_z, 2 * CHUNKS)

            def rows_1(n, u, t):
                pe.wait_ge(s_h, pairs_to(u, t) * 2)
                wait(pe, s_rowev, n - (DEPTH - 1))
                for j in range(2):
                    for k in range(2):
                        last = nc.tensor.matmul(ps[:, u, j * HID:(j + 1) * HID], h_stage[:, u, k, j * P:(j + 1) * P],
                                                w1[:, 0, k, :], start=(k == 0), stop=(k == 1))
                last.then_inc(s_rowmm, 1)
            each_chunk(pe, rows_1)
            pe.wait_ge(s_rowev, CHUNKS)
            sum_edges(1)

            def rows_2(n, u, t):
                pe.wait_ge(s_h2, pairs_to(u, t) * 2)
                wait(pe, s_pev, n - (DEPTH - 1))
                for j in range(2):
                    for k in range(2):
                        last = nc.tensor.matmul(ps[:, u, j * OUT_C:(j + 1) * OUT_C], h_stage[:, u, k, j * P:(j + 1) * P],
                                                w2[:, k, 0:OUT_C], start=(k == 0), stop=(k == 1))
                last.then_inc(s_pmm, 1)
            each_chunk(pe, rows_2)
            pe.wait_ge(s_pev, CHUNKS)
            sum_edges(2)

            def transpose_result(n, u, t):
                pe.wait_ge(s_fin, pairs_to(u, t))
                wait(pe, s_res, pairs_to(u, t) - DEPTH // 2)
                for j in range(2):
                    last = nc.tensor.transpose(ps[:, u, j * P:(j + 1) * P], h_stage[:, u, 0, j * P:(j + 1) * P],
                                               ident[:, :])
                last.then_inc(s_finT, 1)
            each_chunk(pe, transpose_result)

        @block.vector
        def _(dve):
            V = nc.vector
            done = {s_dve: 0, s_sort: 0}

            def link(ins, s=s_dve):
                done[s] += 1
                ins.then_inc(s, 1)
                dve.wait_ge(s, done[s])

            dve.sem_inc(s_acc, PER_IT)
            dve.sem_inc(s_own_acc, 1)
            dve.wait_ge(s_const, 6)
            link(V.tensor_scalar(ident[:, :], iota_row[:, :], part_col[:, 0:1], None, ALU.is_equal))

            dve.wait_ge(s_dst, 48)
            dst_tiles = dst_nat.rearrange("p (c e) -> p c e", e=P)
            link(V.tensor_scalar(first_node[:, :], dst_tiles[:, :, 0], float(PADDED - P), None, ALU.min))

            def places_in_windows(last_one):
                for c in range(KCH):
                    ins = V.tensor_scalar(rel_f[:, c * P:(c + 1) * P], dst_nat[:, c * P:(c + 1) * P],
                                          first_node[:, c:c + 1], None, ALU.subtract)
                last_one(ins)
            places_in_windows(link)

            link(V.tensor_scalar(inside, rel_f, 0.0, None, ALU.is_ge))
            link(V.scalar_tensor_tensor(out=inside, in0=rel_f, scalar=float(P), in1=inside, op0=ALU.is_lt, op1=ALU.mult))
            V.reduce_sum(inside_sum, inside, mybir.AxisListType.X).then_inc(s_insides, 1)
            dve.wait_ge(s_total, 1)
            V.tensor_scalar(outside[:, :], ps[:, 0, 0:1], -1.0, float(EDGES), ALU.mult, ALU.add).then_inc(s_outside, 1)
            with if_irregular(dve):
                dve.wait_ge(s_by_edge, 32)
                dve.wait_ge(s_src, 48)
                V.tensor_scalar(is_before, iota_row[:, :], part_col[:, 0:1], None, ALU.is_gt)
                V.tensor_copy(bucket_no, iota_row[:, 0:BUCKETS])
                V.memset(counts, 0.0)
                link(V.tensor_scalar(bucket_i, dst_by_edge, P.bit_length() - 1, None, ALU.arith_shift_right), s_sort)
                link(V.tensor_scalar(bucket, bucket_i, float(BUCKETS - 1), None, ALU.min), s_sort)
                with dve.Fori(0, TAB_ROWS) as t:
                    V.tensor_scalar(in_bucket, bucket_no, bucket[:, ds(t, 1)], None, ALU.is_equal).then_inc(s_onehot, 1)
                    dve.wait_ge(s_tally, t + 1)
                    V.tensor_tensor(counts, counts, ps[:, 0, 0:BUCKETS], ALU.add).then_inc(s_tallied, 1)
                    dve.wait_ge(s_tallied, t + 1)
                link(V.tensor_tensor_scan(base, ones[:, 0:BUCKETS], counts, 0.0, ALU.mult, ALU.add), s_sort)
                link(V.tensor_tensor(base, base, counts, ALU.subtract), s_sort)
                with dve.Fori(TAB_ROWS, 2 * TAB_ROWS) as t:
                    V.tensor_scalar(in_bucket, bucket_no, bucket[:, ds(t - TAB_ROWS, 1)], None,
                                    ALU.is_equal).then_inc(s_onehot, 1)
                    dve.wait_ge(s_tally, t + 1)
                    V.tensor_tensor(before, base, ps[:, 1, 0:BUCKETS], ALU.add).then_inc(s_tallied, 1)
                    dve.wait_ge(s_tallied, t * 4 - (4 * TAB_ROWS - TAB_ROWS - 1))
                    V.tensor_tensor(base, base, ps[:, 0, 0:BUCKETS], ALU.add)
                    V.tensor_tensor(earlier, before, in_bucket, ALU.mult).then_inc(s_tallied, 1)
                    dve.wait_ge(s_tallied, t * 4 - (4 * TAB_ROWS - TAB_ROWS - 2))
                    V.reduce_sum(place, earlier, mybir.AxisListType.X).then_inc(s_tallied, 1)
                    V.tensor_copy(moved[:, 0:1], src_by_edge[:, ds(t - TAB_ROWS, 1)])
                    V.tensor_copy(moved[:, 1:2], dst_by_edge[:, ds(t - TAB_ROWS, 1)])
                    dve.wait_ge(s_tallied, t * 4 - (4 * TAB_ROWS - TAB_ROWS - 3))
                    V.tensor_copy(place_i, place).then_inc(s_tallied, 1)
                    dve.wait_ge(s_tallied, t * 4 - (4 * TAB_ROWS - TAB_ROWS - 4))
                    dve.sem_inc(s_place, 1)
                    dve.wait_ge(s_moved, t * 32 - (TAB_ROWS * 32 - 32))

                dve.wait_ge(s_firsts, 16)
                link(V.tensor_copy(firsts_f[:, :], firsts[:, :]), s_sort)
                for c in range(KCH):
                    V.tensor_scalar(starts_below[:, c, :], block_end[:, :], firsts_f[:, c:c + 1], None,
                                    ALU.is_gt).then_inc(s_cmp, 1)
                dve.wait_ge(s_counts, 1)
                link(V.tensor_scalar(ends[:, :], ps[:, 0, 0:BLOCKS - 1], 1.0, None, ALU.max), s_sort)
                link(V.tensor_tensor(ends[:, :], ends[:, :], block_no[:, :], ALU.add), s_sort)
                for c in range(KCH):
                    left = V.tensor_scalar(below[:, c, :], ends[:, :], step_no[:, c:c + 1], 0.0, ALU.is_le, ALU.add,
                                           accum_out=block_of[:, c:c + 1])
                    if c == KCH - 1:
                        link(left, s_sort)
                link(V.tensor_scalar(first_node[:, :], block_of[:, :], float(P), None, ALU.mult), s_sort)
                link(V.tensor_tensor(tile_no[:, :], step_no[:, :], block_of[:, :], ALU.subtract), s_sort)
                dve.sem_inc(s_ids, 1)
                dve.wait_ge(s_nat, 16 * 2 * KCH)
                places_in_windows(lambda ins: link(ins, s_sort))

            link(V.tensor_copy(first_node_i[:, :], first_node[:, :]))
            dve.sem_inc(s_windows, 1)
            dve.wait_ge(s_src, 48)
            V.tensor_copy(src_f, src_nat).then_inc(s_natf, 1)
            def layer_norm(g):
                dve.wait_ge(s_x[g], 32 if g == GROUPS - 1 else 16)
                first, end = group(g)

                def block_stats(into, blocks, count):
                    for j in range(count):
                        V.bn_stats(into[:, j, :], blocks[:, j, :]).then_inc(s_lnst, 1)
                with dve.Fori(first // DEPTH, end // DEPTH) as q:
                    block_stats(stats[:, ds(q * (2 * DEPTH), 2 * DEPTH), :], x_nat[:, ds(q * (2 * DEPTH), 2 * DEPTH), :],
                                2 * DEPTH)
                left = 2 * (end % DEPTH)
                block_stats(stats[:, 2 * end - left:2 * end, :], x_nat[:, 2 * end - left:2 * end, :], left)
                first, end = 2 * first, 2 * end
                dve.wait_ge(s_lnst, end)
                mean_g, half_diff = mv[:, first:end, 0], mv[:, first:end, 1]
                rstd_g, stats_g = rstd[:, first:end], stats[:, first:end]
                link(V.tensor_tensor(mean_g, stats_g[:, :, 1], stats_g[:, :, 4], ALU.add))
                link(V.tensor_scalar(mean_g, mean_g, 0.5, None, ALU.mult))
                link(V.tensor_tensor(half_diff, mean_g, stats_g[:, :, 4], ALU.subtract))
                link(V.tensor_tensor(half_diff, half_diff, half_diff, ALU.mult))
                link(V.tensor_tensor(rstd_g, stats_g[:, :, 2], stats_g[:, :, 5], ALU.add))
                link(V.scalar_tensor_tensor(out=rstd_g, in0=rstd_g, scalar=1.0 / IN_C, in1=half_diff,
                                            op0=ALU.mult, op1=ALU.add))
                V.tensor_scalar(rstd_g, rstd_g, EPS, None, ALU.add).then_inc(s_var, 1)
                dve.wait_ge(s_sd, g + 1)
                link(V.reciprocal(rstd_g, rstd_g))
                V.scalar_tensor_tensor(out=nbias[:, first:end], in0=mean_g, scalar=-1.0, in1=rstd_g,
                                       op0=ALU.mult, op1=ALU.mult).then_inc(s_lncoef, 1)

            def keep_h0T(n, u, t):
                dve.wait_ge(s_h0T, n + 1)
                V.tensor_copy(big[:, 0, ds(n * CH, CH)], ps[:, u, 0:CH]).then_inc(s_h0ev, 1)

            layer_norm(0)
            flat_ps = ps[:, :, :].rearrange("p a b -> p (a b)")
            for k, to in enumerate((idx_all, rel_all)):
                dve.wait_ge(s_edgeT, k + 1)
                V.tensor_copy(to[:, :], flat_ps[:, k * 2048:k * 2048 + STEPS]).then_inc(s_edges, 1)

            each_chunk(dve, keep_h0T, before=lambda g: layer_norm(g + 1) if g + 1 < GROUPS else None)

            for g in range(GROUPS):
                first, end = group(g)
                dve.wait_ge(s_h0, 2 * end)
                V.memset(big[:, 1, first * CH:end * CH], 0.0).then_inc(s_zero, 1)
            dve.wait_ge(s_node_row, 16)
            dve.wait_ge(s_zero, GROUPS + 1)

            def hot(layer, i, h, j, node):
                if j == 0:
                    dve.wait_ge(s_sum, half_free(layer, h, i))
                k = h * HALF + j
                rel = rel_all[:, ds(i * IN_TURN[layer] + k, 1)]
                if layer == 0:
                    ins = V.tensor_scalar(onehot[:, k, :], iota_row[:, :], rel, None, ALU.is_equal)
                else:
                    ins = V.scalar_tensor_tensor(out=onehot[:, k, :], in0=iota_row[:, :], scalar=rel,
                                                 in1=big[:, 2, ds(node, P)], op0=ALU.is_equal, op1=ALU.mult)
                if j == in_half(layer, h) - 1:
                    ins.then_inc(s_hot, 1)

            def accumulate(layer, i, h, j, node):
                if j == 0:
                    dve.wait_ge(s_sum, half_free(layer, h, i) + 2)
                k = h * HALF + j
                dve.wait_ge(s_acc, i * PER_IT + (PER_IT * BASE[layer] + PER_IT + k))
                step = ps[:, k // 2, (k % 2) * 256:(k % 2) * 256 + 256]
                if layer == 2:
                    sums = big[:, 0, ds(node, P)]
                    V.tensor_tensor(sums, sums, step[:, 0:P], ALU.add).then_inc(s_acc, 1)
                else:
                    first = 1 if layer == 0 else 0
                    sums = big[:, first:first + 2, ds(node, P)]
                    V.tensor_tensor(sums, sums, step.rearrange("p (m c) -> p m c", m=2), ALU.add).then_inc(s_acc, 1)

            def nodes_of(first, count):
                _, values = nc.values_load_multi_w_load_instructions(
                    node_row[0:1, ds(first, count)], engines=[mybir.EngineType.DVE],
                    min_val=0, max_val=PADDED - P,
                    skip_runtime_bounds_check_because="a window starts at a node or a block, and at most at PADDED - P")
                return values

            def sum_edges(layer):
                n = IN_TURN[layer]

                def hots(i, h, nodes):
                    for j in range(in_half(layer, h)):
                        hot(layer, i, h, j, nodes[h * HALF + j])

                def turn(i, own, last=False):
                    nodes = nodes_of(i * n, n if last else 2 * n)
                    for h in range(2):
                        for j in range(in_half(layer, h)):
                            accumulate(layer, i, h, j, nodes[h * HALF + j])
                            if not last:
                                hot(layer, i + 1, h, j, nodes[n + h * HALF + j])
                    if own:
                        dve.wait_ge(s_acc, i * PER_IT + (PER_IT * BASE[layer] + PER_IT + n))
                        part = ps[:, 7, 256:512]
                        if layer == 1:
                            sums = big[:, 0:2, ds(i * P, P)]
                            V.tensor_tensor(sums, sums, part.rearrange("p (m c) -> p m c", m=2), ALU.add).then_inc(s_acc, 1)
                        else:
                            sums = big[:, 0, ds(i * P, P)]
                            V.tensor_tensor(sums, sums, part[:, P:2 * P], ALU.add).then_inc(s_own_acc, 1)
                            dve.wait_ge(s_own_acc, i + 2)
                    elif n < PER_IT:
                        dve.sem_inc(s_acc, PER_IT - n)

                nodes = nodes_of(0, n)
                if layer:
                    dve.wait_ge(s_tables, layer + 1)
                for h in range(2):
                    hots(0, h, nodes)
                turns = ITERS[layer]
                with dve.Fori(0, min(BLOCKS, turns - 1)) as i:
                    turn(i, layer > 0)
                if turns - 1 > BLOCKS:
                    with dve.Fori(BLOCKS, turns - 1) as i:
                        turn(i, False)
                turn(turns - 1, layer > 0 and turns == BLOCKS, last=True)
                dve.wait_ge(s_acc, PER_IT + PER_IT * BASE[layer + 1])
                with if_irregular(dve):
                    with dve.Fori(0, LATE[layer]) as t:
                        node = nodes_of(t + MAIN[layer], 1)[0]
                        count = t + (LATE_BASE[layer] + 1)
                        V.tensor_copy(idx_now[:, 0, 0:1], idx_all[:, ds(t + MAIN[layer], 1)]).then_inc(s_late_idx, 1)
                        rel = rel_all[:, ds(t + MAIN[layer], 1)]
                        if layer == 0:
                            V.tensor_scalar(onehot[:, 0, :], iota_row[:, :], rel, None, ALU.is_equal).then_inc(s_late_hot, 1)
                        else:
                            V.scalar_tensor_tensor(out=onehot[:, 0, :], in0=iota_row[:, :], scalar=rel,
                                                   in1=big[:, 2, ds(node, P)], op0=ALU.is_equal,
                                                   op1=ALU.mult).then_inc(s_late_hot, 1)
                        dve.wait_ge(s_late_sum, count)
                        sections, step = (slice(0, 1), ps[:, 0, 0:P]) if layer == 2 else \
                            (slice(1, 3) if layer == 0 else slice(0, 2), ps[:, 0, 0:2 * P])
                        sums = big[:, sections, ds(node, P)]
                        V.tensor_tensor(sums, sums, step.rearrange("p (m c) -> p m c", c=P), ALU.add).then_inc(s_late_acc, 1)
                        dve.wait_ge(s_late_acc, count)
                dve.sem_inc(s_summed, 1)

            sum_edges(0)

            dve.wait_ge(s_degree, 16)
            link(V.tensor_scalar(degrees[:, :], degrees[:, :], 1.0, None, ALU.max))
            V.reciprocal(degrees[:, :], degrees[:, :]).then_inc(s_inv, 1)

            def value_stats(part, n, count=1):
                c = LAST_COLS if last_chunk(n) else count * CH
                into, values = stats[:, ds(part * 2, 2), :], big[:, 0:2, ds(n * CH, c)]
                for m in range(2):
                    V.bn_stats(into[:, m, :], values[:, m, :]).then_inc(s_bnst, 1)

            LAG = 3

            def mean_and_stats(n, u, t):
                both = big[:, 1:3, ds(n * CH, CH)]
                V.tensor_tensor(both[:, 0, :], both[:, 0, :], both[:, 1, :], ALU.mult).then_inc(s_mean, 1)
                if not isinstance(n, int) or n >= LAG:
                    dve.wait_ge(s_z, (n - (LAG - 1)) * 2)
                    value_stats(n - LAG, n - LAG)
            each_chunk(dve, mean_and_stats, before=lambda g: dve.wait_ge(s_inv_all[g], 16))
            for n in range(CHUNKS - LAG, CHUNKS):
                dve.wait_ge(s_z, (n + 1) * 2)
                value_stats(n, n)

            def batch_norm(layer):
                parts = (CHUNKS, (CHUNKS + 1) // 2)
                dve.wait_ge(s_bnst, 2 * sum(parts[:layer + 1]))
                for m in range(2):
                    link(V.bn_aggr(bn_mv[:, m, :],
                                   stats[:, 0:2 * parts[layer], :].rearrange("p (n m) s -> p m n s", m=2)[:, m]))
                V.tensor_scalar(bn_tmp[:, :], bn_mv[:, :, 1], EPS, None, ALU.add).then_inc(s_bnvar, 1)
                dve.wait_ge(s_bnsd, layer + 1)
                link(V.reciprocal(bn_tmp[:, :], bn_tmp[:, :]))
                link(V.tensor_tensor(bn_scale[:, :], bn_tmp[:, :], cols[:, 3 * layer + 1, :], ALU.mult))
                link(V.tensor_tensor(bn_tmp[:, :], bn_mv[:, :, 0], bn_scale[:, :], ALU.mult))
                V.tensor_tensor(bn_shift[:, :], cols[:, 3 * layer + 2, :], bn_tmp[:, :], ALU.subtract).then_inc(s_bn, 1)
            dve.wait_ge(s_weights, 16 * 13)
            batch_norm(0)

            def put_bias(n, m, bias, done):
                V.tensor_scalar(big[:, m, ds(n * CH, CH)].rearrange("p (j c) -> p j c", j=2),
                                ones[:, :].rearrange("p (a c) -> p a c", a=1).to_broadcast([P, 2, P]), bias, None,
                                ALU.mult).then_inc(done, 1)

            def keep_rows_1(n, u, t):
                dve.wait_ge(s_rowmm, n + 1)
                v = u % ROW_DEPTH
                wait(dve, s_row_out[v // 2], (t * (DEPTH // ROW_DEPTH) + u // ROW_DEPTH) * 16)
                V.tensor_copy(row_stage[1][:, 2 * v:2 * v + 2, :].rearrange("p j c -> p (j c)"),
                              ps[:, u, :]).then_inc(s_rowev, 1)
                for m in range(2):
                    put_bias(n, m, cols[:, 3, m:m + 1], s_bias)
            each_chunk(dve, keep_rows_1)
            dve.wait_ge(s_bias, 2 * CHUNKS)
            sum_edges(1)

            each_pair(dve, lambda n, u, t, count: value_stats(pairs_to(u, t) - 1, n, count))
            batch_norm(1)

            def keep_rows_2(n, u, t):
                dve.wait_ge(s_pmm, n + 1)
                v = u % ROW_DEPTH
                wait(dve, s_p_out[v // 2], (t * (DEPTH // ROW_DEPTH) + u // ROW_DEPTH) * 16)
                V.tensor_copy(row_stage[2][:, 2 * v:2 * v + 2, :].rearrange("p j c -> p (j c)"),
                              ps[:, u, 0:CH]).then_inc(s_pev, 1)
                put_bias(n, 0, bl2_col[:, 0:1], s_bias2)
            each_chunk(dve, keep_rows_2)
            dve.wait_ge(s_bias2, CHUNKS)
            sum_edges(2)

            dve.wait_ge(s_x_again, 16 * (CHUNKS + 1))

            def add_result(n, u, t, count):
                dve.wait_ge(s_finT, n + count)
                here = big[:, 1, ds(n * CH, count * CH)].rearrange("p (j c) -> p j c", c=CH)
                V.tensor_tensor(here, here, ps[:, u:u + count, 0:CH], ALU.add).then_inc(s_res, 1)
            each_pair(dve, add_result)


_INS = ["x", "src", "dst", "L0_gnn_Wl0", "L0_gnn_bl0", "L0_gnn_Wr0", "L0_gnn_g0", "L0_gnn_b0", "L0_gnn_Wl1",
        "L0_gnn_bl1", "L0_gnn_Wr1", "L0_gnn_g1", "L0_gnn_b1", "L0_gnn_Wl2", "L0_gnn_bl2", "L0_gnn_Wr2"]


def kernel(**inputs):
    import numpy as _np
    import concourse.bacc as _bacc
    from concourse import mybir as _mybir
    from concourse.bass_utils import run_bass_kernel_spmd as _run

    nc = _bacc.Bacc("TRN2", target_bir_lowering=False, num_devices=1)
    arrays, args = {}, []
    for name in _INS:
        a = _np.ascontiguousarray(inputs[name])
        arrays[f"in_{name}"] = a
        args.append(nc.dram_tensor(f"in_{name}", a.shape, _mybir.dt.from_np(a.dtype), kind="ExternalInput").ap())
    args.append(nc.dram_tensor("out_0", (NODES, OUT_C), _mybir.dt.float32, kind="ExternalOutput").ap())
    gnn_kernel(nc, *args)
    r = _run(nc, [arrays], core_ids=[0])
    return r.results[0]["out_0"]
```
